# Optimizing a Trainium2 kernel written in Bass

```python
import numpy as np
import jax
import jax.numpy as jnp

def _softmax(x, axis=-1):
    return jax.nn.softmax(x, axis=axis)

def _gelu(x):
    return jax.nn.gelu(x, approximate=True)

def _silu(x):
    return jax.nn.silu(x)

def _sigmoid(x):
    return jax.nn.sigmoid(x)

def _layernorm(x, axis=-1, eps=1e-05):
    m = jnp.mean(x, axis=axis, keepdims=True)
    v = jnp.var(x, axis=axis, keepdims=True)
    return (x - m) / jnp.sqrt(v + eps)

def _scatter_add(tgt, idx, src, axis=0):
    return tgt.at[idx].add(src)

def _segment_sum(src, seg, n):
    return jax.ops.segment_sum(src, seg, n)
kernel_name = 'mk_macaron_d1_jaxref_r8_647866'

def setup_inputs(seed: int=0):
    np.random.seed(seed)
    _w = jnp.asarray

    def _L0_attn_setup():
        import jax, jax.numpy as jnp
        import numpy as np
        HID = 256
        H = 16
        QLR = 192
        KVLR = 64
        DN = 128
        DR = 64
        DV = 128
        DQ = DN + DR
        B = 2
        S = 256
        THETA = 10000.0
        EPS = 1e-06

        def rms_norm(x, w, eps=EPS):
            x32 = x.astype(jnp.float32)
            var = jnp.mean(x32 * x32, axis=-1, keepdims=True)
            return (w * (x32 * jax.lax.rsqrt(var + eps))).astype(x.dtype)

        def rotate_half(x):
            x1, x2 = jnp.split(x, 2, axis=-1)
            return jnp.concatenate((-x2, x1), axis=-1)

        def rope_tables(seq_len, dim, base=THETA):
            inv_freq = 1.0 / base ** (jnp.arange(0, dim, 2, dtype=jnp.float32) / dim)
            t = jnp.arange(seq_len, dtype=jnp.float32)
            freqs = jnp.outer(t, inv_freq)
            emb = jnp.concatenate((freqs, freqs), -1)
            return (jnp.cos(emb), jnp.sin(emb))
        key = jax.random.key(seed)
        ks = jax.random.split(key, 8)
        sd = lambda fan_in: 1.0 / np.sqrt(fan_in)
        return {'hidden_states': jax.random.normal(ks[0], (B, S, HID), jnp.float32), 'w_qa': jax.random.normal(ks[1], (QLR, HID), jnp.float32) * sd(HID), 'q_a_ln_w': jnp.ones((QLR,), jnp.float32), 'w_qb': jax.random.normal(ks[2], (H * DQ, QLR), jnp.float32) * sd(QLR), 'w_kva': jax.random.normal(ks[3], (KVLR + DR, HID), jnp.float32) * sd(HID), 'kv_a_ln_w': jnp.ones((KVLR,), jnp.float32), 'w_kvb': jax.random.normal(ks[4], (H * (DN + DV), KVLR), jnp.float32) * sd(KVLR), 'w_o': jax.random.normal(ks[5], (HID, H * DV), jnp.float32) * sd(H * DV)}
    _L0_attn_in = _L0_attn_setup()

    def _L0_ffn_setup():
        import jax, jax.numpy as jnp
        import numpy as np
        HIDDEN = 256
        N_EXPERTS = 8
        N_SHARED = 2
        TOP_K = 2
        MOE_FF = 176
        SHARED_FF = N_SHARED * MOE_FF
        SCALE = 2.5
        BATCH, SEQ = (2, 128)
        key = jax.random.key(seed)
        ks = jax.random.split(key, 8)
        s = 0.02
        return {'hidden_states': jax.random.normal(ks[0], (BATCH, SEQ, HIDDEN), jnp.float32), 'gate_w': jax.random.normal(ks[1], (N_EXPERTS, HIDDEN), jnp.float32) * s, 'shared_wg': jax.random.normal(ks[2], (SHARED_FF, HIDDEN), jnp.float32) * s, 'shared_wu': jax.random.normal(ks[3], (SHARED_FF, HIDDEN), jnp.float32) * s, 'shared_wd': jax.random.normal(ks[4], (HIDDEN, SHARED_FF), jnp.float32) * s, 'exp_wg': jax.random.normal(ks[5], (N_EXPERTS, MOE_FF, HIDDEN), jnp.float32) * s, 'exp_wu': jax.random.normal(ks[6], (N_EXPERTS, MOE_FF, HIDDEN), jnp.float32) * s, 'exp_wd': jax.random.normal(ks[7], (N_EXPERTS, HIDDEN, MOE_FF), jnp.float32) * s}
    _L0_ffn_in = _L0_ffn_setup()
    _d = {'L0_attn_hidden_states': _L0_attn_in['hidden_states'], 'L0_attn_w_qa': _L0_attn_in['w_qa'], 'L0_attn_q_a_ln_w': _L0_attn_in['q_a_ln_w'], 'L0_attn_w_qb': _L0_attn_in['w_qb'], 'L0_attn_w_kva': _L0_attn_in['w_kva'], 'L0_attn_kv_a_ln_w': _L0_attn_in['kv_a_ln_w'], 'L0_attn_w_kvb': _L0_attn_in['w_kvb'], 'L0_attn_w_o': _L0_attn_in['w_o'], 'L0_ffn_gate_w': _L0_ffn_in['gate_w'], 'L0_ffn_shared_wg': _L0_ffn_in['shared_wg'], 'L0_ffn_shared_wu': _L0_ffn_in['shared_wu'], 'L0_ffn_shared_wd': _L0_ffn_in['shared_wd'], 'L0_ffn_exp_wg': _L0_ffn_in['exp_wg'], 'L0_ffn_exp_wu': _L0_ffn_in['exp_wu'], 'L0_ffn_exp_wd': _L0_ffn_in['exp_wd']}
    _x0 = _d['L0_attn_hidden_states']
    _d['L0_attn_hidden_states'] = jax.random.normal(jax.random.fold_in(jax.random.key(seed), 1), (8, 256, 256), dtype=_x0.dtype)
    del _x0
    return _d

def reference(L0_attn_hidden_states, L0_attn_w_qa, L0_attn_q_a_ln_w, L0_attn_w_qb, L0_attn_w_kva, L0_attn_kv_a_ln_w, L0_attn_w_kvb, L0_attn_w_o, L0_ffn_gate_w, L0_ffn_shared_wg, L0_ffn_shared_wu, L0_ffn_shared_wd, L0_ffn_exp_wg, L0_ffn_exp_wu, L0_ffn_exp_wd):

    def _L0_attn_ref(hidden_states, w_qa, q_a_ln_w, w_qb, w_kva, kv_a_ln_w, w_kvb, w_o):
        import jax, jax.numpy as jnp
        import numpy as np
        HID = 256
        H = 16
        QLR = 192
        KVLR = 64
        DN = 128
        DR = 64
        DV = 128
        DQ = DN + DR
        B = 2
        S = 256
        THETA = 10000.0
        EPS = 1e-06

        def rms_norm(x, w, eps=EPS):
            x32 = x.astype(jnp.float32)
            var = jnp.mean(x32 * x32, axis=-1, keepdims=True)
            return (w * (x32 * jax.lax.rsqrt(var + eps))).astype(x.dtype)

        def rotate_half(x):
            x1, x2 = jnp.split(x, 2, axis=-1)
            return jnp.concatenate((-x2, x1), axis=-1)

        def rope_tables(seq_len, dim, base=THETA):
            inv_freq = 1.0 / base ** (jnp.arange(0, dim, 2, dtype=jnp.float32) / dim)
            t = jnp.arange(seq_len, dtype=jnp.float32)
            freqs = jnp.outer(t, inv_freq)
            emb = jnp.concatenate((freqs, freqs), -1)
            return (jnp.cos(emb), jnp.sin(emb))
        b, s, _ = hidden_states.shape
        scale = DQ ** (-0.5)
        cos, sin = rope_tables(s, DR)
        cq = rms_norm(hidden_states @ w_qa.T, q_a_ln_w)
        q = (cq @ w_qb.T).reshape(b, s, H, DQ).transpose(0, 2, 1, 3)
        q_nope, q_pe = (q[..., :DN], q[..., DN:])
        q_pe = q_pe * cos + rotate_half(q_pe) * sin
        ckv = hidden_states @ w_kva.T
        k_pe = ckv[..., KVLR:].reshape(b, s, 1, DR).transpose(0, 2, 1, 3)
        k_pe = k_pe * cos + rotate_half(k_pe) * sin
        ckv_l = rms_norm(ckv[..., :KVLR], kv_a_ln_w)
        kv = (ckv_l @ w_kvb.T).reshape(b, s, H, DN + DV).transpose(0, 2, 1, 3)
        k_nope, v = (kv[..., :DN], kv[..., DN:])
        q_full = jnp.concatenate([q_nope, q_pe], axis=-1)
        k_full = jnp.concatenate([k_nope, jnp.broadcast_to(k_pe, (b, H, s, DR))], axis=-1)
        scores = jnp.einsum('bhqd,bhkd->bhqk', q_full, k_full) * scale
        causal = jnp.triu(jnp.ones((s, s), dtype=bool), k=1)
        scores = jnp.where(causal, -jnp.inf, scores)
        attn = jax.nn.softmax(scores.astype(jnp.float32), axis=-1).astype(q_full.dtype)
        out = jnp.einsum('bhqk,bhkd->bhqd', attn, v)
        out = out.transpose(0, 2, 1, 3).reshape(b, s, H * DV)
        return out @ w_o.T

    def _L0_ffn_ref(hidden_states, gate_w, shared_wg, shared_wu, shared_wd, exp_wg, exp_wu, exp_wd):
        import jax, jax.numpy as jnp
        import numpy as np
        HIDDEN = 256
        N_EXPERTS = 8
        N_SHARED = 2
        TOP_K = 2
        MOE_FF = 176
        SHARED_FF = N_SHARED * MOE_FF
        SCALE = 2.5
        BATCH, SEQ = (2, 128)
        B, S, D = hidden_states.shape
        T = B * S
        xf = hidden_states.reshape(T, D)
        scores = jax.nn.sigmoid(xf @ gate_w.T)
        topk_w, topk_idx = jax.lax.top_k(scores, TOP_K)
        topk_w = topk_w / (topk_w.sum(axis=-1, keepdims=True) + 1e-20)
        topk_w = topk_w * SCALE
        shared_out = jax.nn.silu(xf @ shared_wg.T) * (xf @ shared_wu.T) @ shared_wd.T
        h = jax.nn.silu(jnp.einsum('td,efd->etf', xf, exp_wg)) * jnp.einsum('td,efd->etf', xf, exp_wu)
        all_out = jnp.einsum('etf,edf->etd', h, exp_wd)
        picked = all_out[topk_idx, jnp.arange(T)[:, None]]
        routed_out = (topk_w[..., None] * picked).sum(axis=1)
        return (shared_out + routed_out).reshape(B, S, D)
    x = L0_attn_hidden_states
    x = x + 0.5 * _L0_ffn_ref(_layernorm(x, axis=-1), L0_ffn_gate_w, L0_ffn_shared_wg, L0_ffn_shared_wu, L0_ffn_shared_wd, L0_ffn_exp_wg, L0_ffn_exp_wu, L0_ffn_exp_wd)
    x = x + _L0_attn_ref(_layernorm(x, axis=-1), L0_attn_w_qa, L0_attn_q_a_ln_w, L0_attn_w_qb, L0_attn_w_kva, L0_attn_kv_a_ln_w, L0_attn_w_kvb, L0_attn_w_o)
    x = x + 0.5 * _L0_ffn_ref(_layernorm(x, axis=-1), L0_ffn_gate_w, L0_ffn_shared_wg, L0_ffn_shared_wu, L0_ffn_shared_wd, L0_ffn_exp_wg, L0_ffn_exp_wu, L0_ffn_exp_wd)
    return x

_drawn_inputs = setup_inputs


def setup_inputs(seed=0):
    import zlib

    import numpy as np

    out = dict(_drawn_inputs(seed))
    spreads = {'L0_attn_q_a_ln_w': (1.0, 0.2), 'L0_attn_kv_a_ln_w': (1.0, 0.2)}
    factors = {'L0_ffn_gate_w': 8.954,
     'L0_ffn_shared_wg': 2.942,
     'L0_ffn_shared_wu': 2.906,
     'L0_ffn_shared_wd': 2.906,
     'L0_ffn_exp_wg': 2.772,
     'L0_ffn_exp_wu': 2.748,
     'L0_ffn_exp_wd': 2.731}
    for name, (base, spread) in spreads.items():
        noise = np.random.default_rng([zlib.crc32(name.encode()), seed]).standard_normal(out[name].shape)
        drawn = base * np.exp(spread * noise) if base else spread * noise
        out[name] = jnp.asarray(drawn.astype(out[name].dtype))
    for name, factor in factors.items():
        out[name] = (out[name] * factor).astype(out[name].dtype)
    return out
```

```python
from contextlib import ExitStack

import numpy as np

import concourse.bass as bass
from concourse import mybir

F32 = mybir.dt.float32
F32R = mybir.dt.float32r
ALU = mybir.AluOpType
ACT = mybir.ActivationFunctionType
AX = mybir.AxisListType

P = 128
HID = 256
KH = HID // P
NSEQ, SEQ = 8, 256
TPS = SEQ // P
NT = NSEQ * TPS
NE, EFF, SFF = 8, 176, 352
FF = NE * EFF + SFF
GW = 512
NG = -(-FF // GW)
GWID = [min(GW, FF - GW * g) for g in range(NG)]
CH = [[(c, min(P, GWID[g] - c)) for c in range(0, GWID[g], P)] for g in range(NG)]
NCH = sum(len(c) for c in CH)
TOPK_SCALE = 2.5
NH, QLR, KVL, DN, DR, DV = 16, 192, 64, 128, 64, 128
HG = 4
NHG = NH // HG
NUNIT = 3
SM_SCALE = float(DN + DR) ** -0.5
LN_EPS, RMS_EPS = 1e-5, 1e-6
QA = QLR + KVL + DR


class Link:

    def __init__(self, eng, sem):
        self.eng, self.sem, self.base, self.n = eng, sem, 0, 0

    def at(self, base):
        self.base, self.n = base, 0

    def __call__(self, ins):
        self.n += 1
        ins.then_inc(self.sem, 1)
        self.eng.wait_ge(self.sem, self.base + self.n)


def build(nc, d, out):
    with ExitStack() as ctx:
        def sb(name, shape, dt=F32, c=ctx):
            return c.enter_context(nc.sbuf_tensor(name, shape, dt))

        def sem(name):
            return ctx.enter_context(nc.semaphore(name))

        x = sb("x", [P, NT, HID])
        wg_h = sb("wg_h", [P, KH, FF], F32R)
        wg_l = sb("wg_l", [P, KH, FF], F32R)
        wu_h = sb("wu_h", [P, KH, FF], F32R)
        wu_l = sb("wu_l", [P, KH, FF], F32R)
        wd_h = sb("wd_h", [P, NCH, HID], F32R)
        wd_l = sb("wd_l", [P, NCH, HID], F32R)
        gate_h = sb("gate_h", [P, KH, NE], F32R)
        gate_l = sb("gate_l", [P, KH, NE], F32R)
        wq1_h = sb("wq1_h", [P, NH * P], F32R)
        wq1_l = sb("wq1_l", [P, NH * P], F32R)
        wq2 = sb("wq2", [P, NH * P], F32R)
        wvo_h = sb("wvo_h", [P, NH // 2, HID], F32R)
        wvo_l = sb("wvo_l", [P, NH // 2, HID], F32R)
        wqa_h = sb("wqa_h", [P, KH, QA], F32R)
        wqa_l = sb("wqa_l", [P, KH, QA], F32R)
        ident = sb("ident", [P, P])
        mask = sb("mask", [P, P])
        tri8 = sb("tri8", [P, NE, NE])
        cos = sb("cos", [P, TPS, DR])
        sin = sb("sin", [P, TPS, DR])
        kvln_row = sb("kvln_row", [P, KVL])
        kvln2 = sb("kvln2", [P, 1])
        qs = sb("qs", [P, 2])
        mhalf = sb("mhalf", [P, 4])
        ebase = sb("ebase", [P, NE])
        gate_raw = sb("gate_raw", [P, KH, NE])
        qs2 = sb("qs2", [P, 2])
        st6 = sb("st6", [P, 6])
        mv = sb("mv", [P, 2])
        ve = sb("ve", [P, 1])
        rstd = sb("rstd", [P, 1])
        xn = sb("xn", [P, 2, HID])

        xh = [sb(f"xh{i}", [P, KH, P], F32R) for i in range(2)]
        xl = [sb(f"xl{i}", [P, KH, P], F32R) for i in range(2)]
        low = ExitStack()
        silu = sb("silu", [P, 2, GW], c=low)
        hid = sb("hid", [P, 2, GW], c=low)
        hth = sb("hth", [P, 2, 4, P], F32R, c=low)
        htl = sb("htl", [P, 2, 4, P], F32R, c=low)
        nl = sb("nl", [P, NE], c=low)
        en = sb("en", [P, NE], c=low)
        en1 = sb("en1", [P, NE], c=low)
        sg = sb("sg", [P, NE], c=low)
        cgt = sb("cgt", [P, NE, NE], c=low)
        cge = sb("cge", [P, NE, NE], c=low)
        cgl = sb("cgl", [P, NE, NE], c=low)
        cbt = sb("cbt", [P, NE, NE], c=low)
        cnt = sb("cnt", [P, NE], c=low)
        msk = sb("msk", [P, NE], c=low)
        den = sb("den", [P, 3], c=low)
        wgt = sb("wgt", [P, 2, NE], c=low)
        stage = ExitStack()
        NRING = 8
        ring = sb("ring", [P, NRING, 1024], c=stage)
        wqa_raw = sb("wqa_raw", [P, KH, QA], c=stage)
        stage.close()
        stage1 = ExitStack()
        wqb_raw = sb("wqb_raw", [P, NH, 2 * P], c=stage1)
        kvbk_raw = sb("kvbk_raw", [P, NH, KVL], c=stage1)
        wabs = sb("wabs", [P, NH, P], c=stage1)
        stage1.close()
        stage2 = ExitStack()
        kvbv_raw = sb("kvbv_raw", [P, NH // 2, 192], c=stage2)
        wo_raw = sb("wo_raw", [P, NH, HID], c=stage2)
        wvo_raw = sb("wvo_raw", [P, NH // 2, HID], c=stage2)
        stage2.close()
        low.close()

        qa = sb("qa", [P, 2, QA])
        ast6 = sb("ast6", [P, 2, 6])
        amv = sb("amv", [P, 2, 2])
        ave = sb("ave", [P, 2])
        arstd = sb("arstd", [P, 2])
        ms = sb("ms", [P, 2, 2])
        mse = sb("mse", [P, 2, 2])
        rr = sb("rr", [P, 2, 2])
        cq = sb("cq", [P, 2, 3, P])
        kr = sb("kr", [P, 2, 2, DR])
        th = [sb(f"th{i}", [P, 3, 2, P], F32R) for i in range(2)]
        tl = [sb(f"tl{i}", [P, 3, 2, P], F32R) for i in range(2)]
        vpad = [[sb(f"vpad{i}{j}", [P, 192]) for j in range(2)] for i in range(2)]
        qsb = sb("qsb", [P, 2, HG, P])
        rt2 = sb("rt2", [P, 2, HG, DR])
        qth = sb("qth", [P, 2, HG, P], F32R)
        qtl = sb("qtl", [P, 2, HG, P], F32R)
        nmax = sb("nmax", [P, 2, HG])
        rsum = sb("rsum", [P, NUNIT, HG])
        rcp = sb("rcp", [P, NUNIT, HG])
        prob = sb("prob", [P, NUNIT, 512])
        pt0 = sb("pt0", [P, HG, SEQ])
        pt1 = sb("pt1", [P, HG, P])
        oth = [sb(f"oth{i}", [P, 2, SEQ], F32R) for i in range(2)]
        otl = [sb(f"otl{i}", [P, 2, SEQ], F32R) for i in range(2)]

        B = [ctx.enter_context(nc.psum_tensor(f"B{i}", [P, 512], F32)) for i in range(8)]

        sp_x = sem("sp_x")
        sp_c = sem("sp_c")
        sp_w = [sem(f"sp_w{i}") for i in range(12)]
        sp_gate = sem("sp_gate")
        sp_qa = sem("sp_qa")
        sp_a1 = sem("sp_a1")
        sp_r1 = sem("sp_r1")
        sp_r2 = sem("sp_r2")
        sp_a2 = sem("sp_a2")
        sp_out = sem("sp_out")
        a_wh = sem("a_wh")
        v_wl = sem("v_wl")
        g_wl = sem("g_wl")
        v_one = sem("v_one")
        v_link = sem("v_link")
        v_turn = sem("v_turn")
        v_st = sem("v_st")
        g_rs = sem("g_rs")
        v_xn = sem("v_xn")
        t_xt = sem("t_xt")
        a_xh = sem("a_xh")
        v_xl = sem("v_xl")
        t_lg = sem("t_lg")
        v_nl = sem("v_nl")
        g_en = sem("g_en")
        v_wt = sem("v_wt")
        t_g = sem("t_g")
        t_u = sem("t_u")
        a_sl = sem("a_sl")
        v_h = sem("v_h")
        t_ht = sem("t_ht")
        a_hh = sem("a_hh")
        v_hl = sem("v_hl")
        t_dn = sem("t_dn")
        v_x = sem("v_x")
        v_pad = sem("v_pad")
        t_w = sem("t_w")
        v_w = sem("v_w")
        a_w = sem("a_w")
        v_wlo = sem("v_wlo")
        v_ast = sem("v_ast")
        g_ars = sem("g_ars")
        v_axn = sem("v_axn")
        t_ax = sem("t_ax")
        a_ax = sem("a_ax")
        v_ax = sem("v_ax")
        t_qa = sem("t_qa")
        a_qa = sem("a_qa")
        a_ms = sem("a_ms")
        v_ms = sem("v_ms")
        g_rr = sem("g_rr")
        v_cq = sem("v_cq")
        t_at = sem("t_at")
        a_at = sem("a_at")
        v_at = sem("v_at")
        t_q = sem("t_q")
        a_q = sem("a_q")
        v_q = sem("v_q")
        g_q = sem("g_q")
        t_qt = sem("t_qt")
        a_qt = sem("a_qt")
        v_qt = sem("v_qt")
        t_s = sem("t_s")
        v_m = sem("v_m")
        a_e = sem("a_e")
        v_r = sem("v_r")
        g_n = sem("g_n")
        t_t = sem("t_t")
        a_t = sem("a_t")
        t_o = sem("t_o")
        a_o = sem("a_o")
        v_o = sem("v_o")
        t_p = sem("t_p")
        v_ux = sem("v_ux")

        units = []
        for g in range(NG):
            units += [("g", g), ("u", g)]
            if g >= 1:
                units.append(("d", g - 1))
        units.append(("d", NG - 1))
        uidx = {u: i for i, u in enumerate(units)}

        def unit_raw(i):
            kind, g = units[i]
            r = ring[:, i % NRING, :]
            if kind == "d":
                n = len(CH[g])
                return r[:, 0:n * HID].rearrange("p (c n) -> p c n", c=n)
            return r[:, 0:KH * GWID[g]].rearrange("p (k n) -> p k n", k=KH)

        def unit_dst(i, lo):
            kind, g = units[i]
            if kind == "d":
                return (wd_l if lo else wd_h)[:, 4 * g:4 * g + len(CH[g]), :]
            w = {"g": (wg_h, wg_l), "u": (wu_h, wu_l)}[kind][lo]
            return w[:, :, GW * g:GW * g + GWID[g]]

        def lo_on_pool(i):
            return units[i][0] == "u"

        DVE_UNITS = [i for i in range(12) if not lo_on_pool(i)]
        POOL_UNITS = [i for i in range(12) if lo_on_pool(i)]

        def wait_unit(eng, key):
            i = uidx[key]
            if lo_on_pool(i):
                eng.wait_ge(g_wl, POOL_UNITS.index(i) + 1)
            else:
                eng.wait_ge(v_wl, DVE_UNITS.index(i) + 2)

        def segments(g):
            lo, hi = GW * g, GW * g + GWID[g]
            segs = [(e * EFF, (e + 1) * EFF, e) for e in range(NE)] + [(NE * EFF, FF, None)]
            return [(max(a, lo) - lo, min(b, hi) - max(a, lo), e) for a, b, e in segs if a < hi and b > lo]

        def unit_par(gi, u):
            return (3 * gi + u) % 2

        def split3(mm, out_, lh, ll, rh, rl, start, stop, **kw):
            mm(out_, lh, rh, start=start, stop=False, **kw)
            mm(out_, lh, rl, start=False, stop=False, **kw)
            return mm(out_, ll, rh, start=False, stop=stop, **kw)

        block = ctx.enter_context(nc.Block())
        out_v = out.rearrange("b (h p) d -> p (b h) d", p=P)
        x_v = d["x"].rearrange("b (h p) d -> p (b h) d", p=P)

        def pairs(eng, first, last, body):
            body(first, first % 2, True, False)
            with eng.Fori(first + 1, last - 1, 2) as i:
                body(i, (first + 1) % 2, False, False)
                body(i + 1, first % 2, False, False)
            body(last, last % 2, False, True)

        @block.sync
        def _(sp):
            sp.dma_start(x[:, 0:2, :], x_v[:, 0:2, :]).then_inc(sp_x, 16)
            for t_, s_ in ((ident, "ident"), (tri8, "tri8"), (mask, "mask"), (cos, "cos"), (sin, "sin"),
                           (kvln_row, "kvln_row"), (kvln2, "kvln2"), (qs, "qln")):
                sp.dma_start(t_[tuple(slice(None) for _ in t_.shape)], d[s_]).then_inc(sp_c, 16)
            sp.dma_start(gate_raw[:, :, :], d["gate"].rearrange("(k p) n -> p k n", p=P)).then_inc(sp_gate, 16)

            def load_unit(i):
                kind, g = units[i]
                if i >= NRING:
                    wait_unit(sp, units[i - NRING])
                if kind == "d":
                    n = sum(w == P for _, w in CH[g])
                    src = d["wd"][GW * g:GW * g + n * P, :].rearrange("(c p) n -> p c n", p=P)
                    sp.dma_start(unit_raw(i)[:, 0:n, :], src).then_inc(sp_w[i], 16)
                    if n < len(CH[g]):
                        w = CH[g][n][1]
                        sp.dma_start(unit_raw(i)[0:w, n, :], d["wd"][GW * g + n * P:FF, :]).then_inc(sp_w[i], 16)
                else:
                    src = d["w" + kind].rearrange("(k p) n -> p k n", p=P)[:, :, GW * g:GW * g + GWID[g]]
                    sp.dma_start(unit_raw(i), src).then_inc(sp_w[i], 16)

            for i in range(2):
                load_unit(i)
            sp.dma_start(x[:, 2:NT, :], x_v[:, 2:NT, :]).then_inc(sp_x, 16)
            for i in range(2, 12):
                load_unit(i)
            sp.dma_start(wqa_raw[:, :, :], d["wqa"].rearrange("(k p) n -> p k n", p=P)).then_inc(sp_qa, 16)
            sp.wait_ge(v_wl, len(DVE_UNITS) + 2)
            sp.wait_ge(g_wl, len(POOL_UNITS))
            sp.dma_start(wqb_raw[:, :, 0:QLR], d["wqbn"]).then_inc(sp_a1, 16)
            sp.dma_start(wqb_raw[:, :, QLR:2 * P], d["wqbn"][:, :, P:QLR]).then_inc(sp_a1, 16)
            sp.dma_start(kvbk_raw[:, :, :], d["kvbk"]).then_inc(sp_a1, 16)
            sp.dma_start(wabs[:, :, KVL:P], d["wqbp"][0:P]).then_inc(sp_r1, 16)
            sp.wait_ge(v_wlo, 1)
            for i in range(2):
                sp.dma_start(wabs[64 * i:64 * i + 64, :, KVL:P], d["wqbp"][P:QLR]).then_inc(sp_r2, 16)
            sp.wait_ge(v_wlo, 2)
            kv = d["kvbv"].rearrange("p (h e) n -> p h e n", e=2)
            sp.dma_start(kvbv_raw[:, :, 0:64], kv[:, :, 0, :]).then_inc(sp_a2, 16)
            sp.dma_start(kvbv_raw[:, :, 128:192], kv[:, :, 1, :]).then_inc(sp_a2, 16)
            sp.dma_start(wo_raw[:, :, :], d["wo"]).then_inc(sp_a2, 16)
            for i in range(4):
                sp.wait_ge(v_x, NT + 4 * i + 4)
                sp.dma_start(out_v[:, 4 * i:4 * i + 4, :], x[:, 4 * i:4 * i + 4, :]).then_inc(sp_out, 16)
            sp.wait_ge(sp_out, 64)

        @block.tensor
        def _(pe):
            mm, tr = nc.tensor.matmul, nc.tensor.transpose

            def ffn(f):
                t0 = NT * f

                def xt(t):
                    pe.wait_ge(v_xn, t + 1)
                    if not (isinstance(t, int) and t == 0):
                        pe.wait_ge(v_nl, t)
                    for k in range(KH):
                        last = tr(B[7][:, k * P:(k + 1) * P], xn[:, 0, k * P:(k + 1) * P], ident[:, :])
                    last.then_inc(t_xt, 1)

                def logits(t, par):
                    pe.wait_ge(v_xl, t + 1)
                    for k in range(KH):
                        last = split3(mm, B[7][:, 256:256 + NE], xh[par][:, k, :], xl[par][:, k, :],
                                      gate_h[:, k, :], gate_l[:, k, :], k == 0, k == KH - 1)
                    last.then_inc(t_lg, 1)

                def up(n, g, par):
                    if not (isinstance(n, int) and n < 2):
                        pe.wait_ge(v_h, n - 1)
                    for w_h, w_l, bank, kind, s_ in ((wg_h, wg_l, B[g % 2], "g", t_g), (wu_h, wu_l, B[2 + g % 2], "u", t_u)):
                        if isinstance(n, int) and n < NG:
                            wait_unit(pe, (kind, g))
                        c = slice(GW * g, GW * g + GWID[g])
                        for k in range(KH):
                            last = split3(mm, bank[:, 0:GWID[g]], xh[par][:, k, :], xl[par][:, k, :],
                                          w_h[:, k, c], w_l[:, k, c], k == 0, k == KH - 1)
                        last.then_inc(s_, 1)

                def ht(n, g):
                    pe.wait_ge(v_h, n + 1)
                    if not (isinstance(n, int) and n < 2):
                        pe.wait_ge(v_hl, n - 1)
                    for i, (c, w) in enumerate(CH[g]):
                        last = tr(B[4 + g % 2][0:w, i * P:(i + 1) * P], hid[:, g % 2, c:c + w], ident[:, :])
                    last.then_inc(t_ht, 1)

                def down(n, g, t):
                    pe.wait_ge(v_hl, n + 1)
                    if isinstance(n, int) and n < NG:
                        wait_unit(pe, ("d", g))
                    if g == 0 and not (isinstance(t, int) and t == 0):
                        pe.wait_ge(v_x, t)
                    for i, (c, w) in enumerate(CH[g]):
                        last = split3(mm, B[6][:, 0:HID], hth[0:w, g % 2, i, :], htl[0:w, g % 2, i, :],
                                      wd_h[0:w, 4 * g + i, :], wd_l[0:w, 4 * g + i, :],
                                      g == 0 and i == 0, g == NG - 1 and i == len(CH[g]) - 1)
                    last.then_inc(t_dn, 1)

                if f == 0:
                    pe.wait_ge(sp_c, 8 * 16)
                    pe.wait_ge(a_wh, 1)
                    pe.wait_ge(v_wl, 1)
                else:
                    pe.wait_ge(v_ux, NSEQ)
                xt(t0)
                logits(t0, 0)

                def tile(i, par, first, last):
                    t = i + t0
                    n = t * NG
                    for g in range(NG):
                        up(n + g, g, par)
                        if g == 1 and not last:
                            xt(t + 1)
                        if g == 2 and not last:
                            logits(t + 1, 1 - par)
                        if not (first and g == 0):
                            ht(n + g - 1, (g - 1) % NG)
                        if not (first and g < 2):
                            down(n + g - 2, (g - 2) % NG, t if g >= 2 else t - 1)

                pairs(pe, 0, NT - 1, tile)
                n = (t0 + NT) * NG
                ht(n - 1, NG - 1)
                down(n - 2, NG - 2, t0 + NT - 1)
                down(n - 1, NG - 1, t0 + NT - 1)

            def attention_weights():
                pe.wait_ge(v_x, NT)
                pe.wait_ge(sp_a1, 3 * 16)
                for c in range(2):
                    for h in range(NH):
                        last = mm(B[2 * c + h // 8][:, (h % 8) * KVL:(h % 8 + 1) * KVL],
                                  wqb_raw[:, h, c * P:(c + 1) * P], kvbk_raw[:, h, :], start=True, stop=True)
                    last.then_inc(t_w, 1)
                pe.wait_ge(sp_a2, 3 * 16)
                pe.wait_ge(v_pad, 1)
                for p in range(NH // 2):
                    for e in range(2):
                        last = mm(B[4 + p // 2][:, (p % 2) * HID:(p % 2 + 1) * HID],
                                  kvbv_raw[:, p, 64 * e:64 * e + P], wo_raw[:, 2 * p + e, :], start=(e == 0), stop=(e == 1))
                last.then_inc(t_w, 1)

            def attention():
                def transpose_x(b):
                    pe.wait_ge(v_axn, b + 1)
                    for j in range(2):
                        for k in range(KH):
                            last = tr(B[6 + j][:, k * P:(k + 1) * P], xn[:, j, k * P:(k + 1) * P], ident[:, :])
                        last.then_inc(t_ax, 1)

                def down_projections(b):
                    for j in range(2):
                        pe.wait_ge(v_ax, 2 * b + j + 1)
                        for k in range(KH):
                            last = split3(mm, B[6 + j][:, 0:QA], xh[j][:, k, :], xl[j][:, k, :],
                                          wqa_h[:, k, :], wqa_l[:, k, :], k == 0, k == KH - 1)
                        last.then_inc(t_qa, 1)

                def transpose_latents(b):
                    pe.wait_ge(v_cq, b + 1)
                    for j in range(2):
                        for k in range(3):
                            last = tr(B[6 + j][:, k * P:(k + 1) * P], cq[:, j, k, :], ident[:, :])
                        last.then_inc(t_at, 1)

                def queries(gi, par, j):
                    cs = slice(512 * gi, 512 * gi + 512)
                    split3(mm, B[6 + j][:, :], th[par][:, 0, j, :], tl[par][:, 0, j, :], wq1_h[:, cs], wq1_l[:, cs],
                           True, False)
                    mm(B[6 + j][:, :], th[par][:, 1, j, :], wq2[:, cs], start=False, stop=False)
                    mm(B[6 + j][:, :], tl[par][:, 1, j, :], wq2[:, cs], start=False, stop=True).then_inc(t_q, 1)

                def transpose_queries(c):
                    for j in range(2):
                        pe.wait_ge(a_q, 2 * c + j + 1)
                        pe.wait_ge(g_q, 2 * c + j + 1)
                        for h in range(HG):
                            last = tr(B[6 + j][:, h * P:(h + 1) * P], qsb[:, j, h, :], ident[:, :])
                        last.then_inc(t_qt, 1)

                def scores(c, gi, u, par):
                    m = 3 * c + u
                    if u == 0:
                        pe.wait_ge(v_qt, 2 * c + 2)
                    if not (isinstance(m, int) and m < 2):
                        pe.wait_ge(a_e, m - 1)
                    j, heads, nk = (0, range(4), 1) if u == 0 else (1, range(2 * u - 2, 2 * u), 2)
                    for i, h in enumerate(heads):
                        last = split3(mm, B[unit_par(gi, u)][:, i * nk * P:(i + 1) * nk * P],
                                      qth[:, j, h, :], qtl[:, j, h, :],
                                      th[par][:, 2, 0:nk, :], tl[par][:, 2, 0:nk, :], True, True)
                    last.then_inc(t_s, 1)

                def transpose_probs(c, gi, u):
                    m = 3 * c + u
                    pe.wait_ge(g_n, m + 1)
                    if not (isinstance(m, int) and m < 2):
                        pe.wait_ge(a_t, m - 1)
                    for i in range(4):
                        src = i if u == 0 else 2 * (i % 2) + i // 2
                        last = tr(B[2 + unit_par(gi, u)][:, i * P:(i + 1) * P],
                                  prob[:, u, src * P:(src + 1) * P], ident[:, :])
                    last.then_inc(t_t, 1)

                def head_outputs(c, gi, par):
                    pe.wait_ge(a_t, 3 * c + 3)
                    if not (isinstance(c, int) and c == 0):
                        pe.wait_ge(v_o, c)
                    o = B[4][:, :].rearrange("p (r q) -> p r q", r=2)
                    for e in range(2):
                        mm(o, vpad[par][0][:, 64 - 64 * e:192 - 64 * e],
                           pt0[:, e::2, :], start=(e == 0), stop=False, skip_group_check=True)
                    for e in range(2):
                        last = mm(o[:, :, P:SEQ], vpad[par][1][:, 64 - 64 * e:192 - 64 * e], pt1[:, e::2, :],
                                  start=False, stop=(e == 1), skip_group_check=True)
                    last.then_inc(t_o, 1)

                def out_projection(c, gi, b):
                    pe.wait_ge(v_o, c + 1)
                    if gi == 0 and not (isinstance(b, int) and b == 0):
                        pe.wait_ge(v_ux, b)
                    for j in range(2):
                        for r in range(2):
                            q = slice(j * P, (j + 1) * P)
                            last = split3(mm, B[5][:, j * HID:(j + 1) * HID], oth[gi % 2][:, r, q], otl[gi % 2][:, r, q],
                                          wvo_h[:, 2 * gi + r, :], wvo_l[:, 2 * gi + r, :],
                                          gi == 0 and j == 0 and r == 0, gi == NHG - 1 and r == 1,
                                          skip_group_check=True)
                    last.then_inc(t_p, 1)

                pe.wait_ge(v_wlo, 6)
                transpose_x(0)
                down_projections(0)
                transpose_latents(0)
                for j in range(2):
                    pe.wait_ge(v_at, j + 1)
                    queries(0, 0, j)
                transpose_queries(0)

                def sequence(b, par, first, last):
                    for gi in range(NHG):
                        c = NHG * b + gi
                        end = last and gi == NHG - 1
                        if gi and not last:
                            pe.wait_ge(v_qt, 2 * c + 2)
                            (transpose_x, down_projections, transpose_latents)[gi - 1](b + 1)
                        scores(c, gi, 0, par)
                        if not (first and gi == 0):
                            transpose_probs(c - 1, (gi - 1) % NHG, 2)
                        for j in range(2):
                            if end:
                                break
                            if gi == 0 or last:
                                pe.wait_ge(v_qt, 2 * c + j + 1)
                            else:
                                pe.wait_ge((v_ax, a_qa, v_at)[gi - 1], 2 * b + j + 3)
                            queries((gi + 1) % NHG, par if gi < NHG - 1 else 1 - par, j)
                        scores(c, gi, 1, par)
                        scores(c, gi, 2, par)
                        if not (first and gi == 0):
                            head_outputs(c - 1, (gi - 1) % NHG, par if gi else 1 - par)
                        if not end:
                            transpose_queries(c + 1)
                        transpose_probs(c, gi, 0)
                        transpose_probs(c, gi, 1)
                        if not (first and gi < 2):
                            out_projection(c - 2, (gi - 2) % NHG, b if gi >= 2 else b - 1)

                pairs(pe, 0, NSEQ - 1, sequence)
                c = NHG * NSEQ - 1
                transpose_probs(c, NHG - 1, 2)
                out_projection(c - 1, NHG - 2, NSEQ - 1)
                head_outputs(c, NHG - 1, (NSEQ - 1) % 2)
                out_projection(c, NHG - 1, NSEQ - 1)

            ffn(0)
            attention_weights()
            attention()
            ffn(1)

        @block.scalar
        def _(act):
            copy, fn = nc.scalar.copy, nc.scalar.activation

            def ffn(f):
                t0 = NT * f

                def high_x(t, par):
                    act.wait_ge(t_xt, t + 1)
                    copy(xh[par][:, :, :], B[7][:, 0:HID].rearrange("p (k n) -> p k n", k=KH)).then_inc(a_xh, 1)

                def high_hidden(n, g):
                    act.wait_ge(t_ht, n + 1)
                    if not (isinstance(n, int) and n < 2):
                        act.wait_ge(t_dn, n - 1)
                    full = sum(w == P for _, w in CH[g])
                    bank = B[4 + g % 2][:, :].rearrange("p (c n) -> p c n", n=P)
                    last = copy(hth[:, g % 2, 0:full, :], bank[:, 0:full, :])
                    if full < len(CH[g]):
                        w = CH[g][full][1]
                        last = copy(hth[0:w, g % 2, full, :], bank[0:w, full, :])
                    last.then_inc(a_hh, 1)

                if f == 1:
                    act.wait_ge(v_ux, NSEQ)
                nc.scalar.preload_act_table(ACT.Silu)
                high_x(t0, 0)

                def tile(i, par, first, last):
                    t = i + t0
                    for g in range(NG):
                        n = t * NG + g
                        act.wait_ge(t_g, n + 1)
                        if not (isinstance(n, int) and n < 2):
                            act.wait_ge(v_h, n - 1)
                        fn(silu[:, g % 2, 0:GWID[g]], B[g % 2][:, 0:GWID[g]], ACT.Silu).then_inc(a_sl, 1)
                        if g == 1 and not last:
                            high_x(t + 1, 1 - par)
                        if not (first and g == 0):
                            high_hidden(n - 1, (g - 1) % NG)

                pairs(act, 0, NT - 1, tile)
                high_hidden((t0 + NT) * NG - 1, NG - 1)

            act.wait_ge(sp_gate, 16)
            copy(gate_h[:, :, :], gate_raw[:, :, :]).then_inc(a_wh, 1)
            for i, (kind, g) in enumerate(units):
                act.wait_ge(sp_w[i], 32 if (kind, g) == ("d", NG - 1) else 16)
                src, dst = unit_raw(i), unit_dst(i, 0)
                full = sum(w == P for _, w in CH[g]) if kind == "d" else KH
                last = copy(dst[:, 0:full, :], src[:, 0:full, :])
                if kind == "d" and full < len(CH[g]):
                    w = CH[g][full][1]
                    last = copy(dst[0:w, full, :], src[0:w, full, :])
                last.then_inc(a_wh, 1)
            act.wait_ge(sp_qa, 16)
            copy(wqa_h[:, :, :], wqa_raw[:, :, :]).then_inc(a_wh, 1)

            ffn(0)

            act.wait_ge(v_w, 1)
            copy(wq1_h[:, :], wabs[:, :, :].rearrange("p h n -> p (h n)")).then_inc(a_w, 1)
            act.wait_ge(v_w, 2)
            copy(wq2[:, :], wabs[:, :, :].rearrange("p h n -> p (h n)")).then_inc(a_w, 1)
            for q in range(4):
                act.wait_ge(v_w, 3 + q)
                copy(wvo_h[:, 2 * q:2 * q + 2, :], wvo_raw[:, 2 * q:2 * q + 2, :]).then_inc(a_w, 1)

            def attention():
                def high_x(b):
                    for j in range(2):
                        act.wait_ge(t_ax, 2 * b + j + 1)
                        copy(xh[j][:, :, :], B[6 + j][:, 0:HID].rearrange("p (k n) -> p k n", k=KH)).then_inc(a_ax, 1)

                def copy_latents(b):
                    for j in range(2):
                        act.wait_ge(t_qa, 2 * b + j + 1)
                        copy(qa[:, j, :], B[6 + j][:, 0:QA]).then_inc(a_qa, 1)

                def mean_squares(b):
                    act.wait_ge(a_qa, 2 * b + 2)
                    for j in range(2):
                        for i, (a, w) in enumerate(((0, QLR), (QLR, KVL))):
                            last = fn(cq[:, j, :, :].rearrange("p k n -> p (k n)")[:, a:a + w], qa[:, j, a:a + w], ACT.Square, scale=float(w) ** -0.5,
                                      accum_out=ms[:, j, i:i + 1])
                    last.then_inc(a_ms, 1)

                def high_latents(b, par):
                    for j in range(2):
                        act.wait_ge(t_at, 2 * b + j + 1)
                        copy(th[par][:, :, j, :], B[6 + j][:, 0:3 * P].rearrange("p (k n) -> p k n", k=3)).then_inc(a_at, 1)

                def copy_queries(c):
                    for j in range(2):
                        act.wait_ge(t_q, 2 * c + j + 1)
                        copy(qsb[:, j, :, 0:KVL],
                             B[6 + j][:, :].rearrange("p (h n) -> p h n", h=HG)[:, :, 0:KVL]).then_inc(a_q, 1)

                def high_queries(c, gi):
                    for j in range(2):
                        act.wait_ge(t_qt, 2 * c + j + 1)
                        copy(qth[:, j, :, :], B[6 + j][:, :].rearrange("p (h n) -> p h n", h=HG)).then_inc(a_qt, 1)

                def exponentials(c, gi, u):
                    m, k = 3 * c + u, unit_par(gi, u)
                    act.wait_ge(v_m, m + 1)
                    if not (isinstance(m, int) and m < NUNIT):
                        act.wait_ge(t_t, m - 2)
                    nh = 4 if u == 0 else 2
                    w = 512 // nh
                    for i in range(nh):
                        last = fn(prob[:, u, i * w:(i + 1) * w], B[k][:, i * w:(i + 1) * w], ACT.Exp,
                                  bias=nmax[:, k, i:i + 1], accum_out=rsum[:, u, i:i + 1])
                    last.then_inc(a_e, 1)

                def copy_probs(c, gi, u):
                    act.wait_ge(t_t, 3 * c + u + 1)
                    bank = B[2 + unit_par(gi, u)][:, :].rearrange("p (h n) -> p h n", h=HG)
                    if u == 0:
                        last = copy(pt0[:, :, 0:P], bank)
                    else:
                        hs = slice(2 * u - 2, 2 * u)
                        copy(pt0[:, hs, P:SEQ], bank[:, 0:2, :])
                        last = copy(pt1[:, hs, :], bank[:, 2:4, :])
                    last.then_inc(a_t, 1)

                def high_outputs(c, gi):
                    act.wait_ge(t_o, c + 1)
                    copy(oth[gi % 2][:, :, :], B[4][:, :].rearrange("p (r q) -> p r q", r=2)).then_inc(a_o, 1)

                act.wait_ge(v_wlo, 6)
                nc.scalar.preload_act_table(ACT.Exp)
                high_x(0)
                copy_latents(0)
                mean_squares(0)
                high_latents(0, 0)
                copy_queries(0)
                high_queries(0, 0)

                def sequence(b, par, first, last):
                    for gi in range(NHG):
                        c = NHG * b + gi
                        end = last and gi == NHG - 1
                        if not last:
                            if gi == 1:
                                high_x(b + 1)
                            if gi == 2:
                                copy_latents(b + 1)
                            if gi == 3:
                                high_latents(b + 1, 1 - par)
                        if not (first and gi == 0):
                            copy_probs(c - 1, (gi - 1) % NHG, 2)
                        exponentials(c, gi, 0)
                        if not end:
                            copy_queries(c + 1)
                        exponentials(c, gi, 1)
                        if gi == 2 and not last:
                            mean_squares(b + 1)
                        exponentials(c, gi, 2)
                        if not (first and gi == 0):
                            high_outputs(c - 1, (gi - 1) % NHG)
                        if not end:
                            high_queries(c + 1, (gi + 1) % NHG)
                        copy_probs(c, gi, 0)
                        copy_probs(c, gi, 1)

                pairs(act, 0, NSEQ - 1, sequence)
                c = NHG * NSEQ - 1
                copy_probs(c, NHG - 1, 2)
                high_outputs(c, NHG - 1)

            attention()
            ffn(1)

        @block.vector
        def _(dve):
            V = nc.vector
            link = Link(dve, v_link)
            linked = [0]

            def minus(out_, a, hi):
                return V.tensor_tensor(out_, a, hi.bitcast(F32), ALU.subtract)

            def ffn(f):
                t0 = NT * f

                def variance(t):
                    V.bn_stats(st6[:, :], x[:, t - t0, :]).then_inc(v_link, 1)
                    link.n += 1
                    dve.wait_ge(v_link, link.base + link.n)
                    dve.sem_inc(v_turn, 1)
                    link(V.bn_aggr(mv[:, :], st6[:, :]))
                    V.tensor_scalar(ve[:, :], mv[:, 1:2], LN_EPS, None, ALU.add).then_inc(v_st, 1)

                def normalise(t):
                    dve.wait_ge(g_rs, t + 1)
                    V.tensor_scalar(xn[:, 0, :], x[:, t - t0, :], mv[:, 0:1], rstd[:, 0:1], ALU.subtract,
                                    ALU.mult).then_inc(v_xn, 1)

                def low_x(t, par):
                    dve.wait_ge(a_xh, t + 1)
                    minus(xl[par][:, :, :], B[7][:, 0:HID].rearrange("p (k n) -> p k n", k=KH),
                          xh[par][:, :, :]).then_inc(v_xl, 1)

                def negate_logits(t):
                    dve.wait_ge(t_lg, t + 1)
                    V.tensor_scalar(nl[:, :], B[7][:, 256:256 + NE], -1.0, None, ALU.mult).then_inc(v_nl, 1)

                def expert_weights(t, par):
                    dve.wait_ge(g_en, t + 1)
                    link(V.tensor_scalar(en1[:, :], en[:, :], 1.0, None, ALU.add))
                    link(V.reciprocal(sg[:, :], en1[:, :]))
                    other = sg[:, :].unsqueeze(1).broadcast_to([P, NE, NE])
                    own = sg[:, :].unsqueeze(2).broadcast_to([P, NE, NE])
                    V.tensor_tensor(cgt[:, :, :], other, own, ALU.is_gt)
                    link(V.tensor_tensor(cge[:, :, :], other, own, ALU.is_ge))
                    link(V.tensor_tensor(cgl[:, :, :], cge[:, :, :], tri8[:, :, :], ALU.mult))
                    link(V.tensor_tensor(cbt[:, :, :], cgl[:, :, :], cgt[:, :, :], ALU.max))
                    link(V.tensor_reduce(cnt[:, :], cbt[:, :, :], AX.X, ALU.add))
                    link(V.scalar_tensor_tensor(msk[:, :], cnt[:, :], 2.0, sg[:, :], ALU.is_lt, ALU.mult,
                                                accum_out=den[:, 0:1]))
                    link(V.tensor_scalar(den[:, 1:2], den[:, 0:1], 1e-20, None, ALU.add))
                    link(V.reciprocal(den[:, 2:3], den[:, 1:2]))
                    V.tensor_scalar(wgt[:, par, :], msk[:, :], den[:, 2:3], TOPK_SCALE, ALU.mult,
                                    ALU.mult).then_inc(v_wt, 1)

                def middle(n, g, par, t):
                    dve.wait_ge(t_u, n + 1)
                    dve.wait_ge(a_sl, n + 1)
                    if g == 0:
                        dve.wait_ge(v_wt, t + 1)
                    if not (isinstance(n, int) and n < 2):
                        dve.wait_ge(t_ht, n - 1)
                    for a, w, e in segments(g):
                        s_, u_ = silu[:, g % 2, a:a + w], B[2 + g % 2][:, a:a + w]
                        if e is None:
                            last = V.tensor_tensor(hid[:, g % 2, a:a + w], s_, u_, ALU.mult)
                        else:
                            last = V.scalar_tensor_tensor(hid[:, g % 2, a:a + w], s_, wgt[:, par, e:e + 1], u_,
                                                          ALU.mult, ALU.mult)
                    last.then_inc(v_h, 1)

                def low_hidden(n, g):
                    dve.wait_ge(a_hh, n + 1)
                    full = sum(w == P for _, w in CH[g])
                    bank = B[4 + g % 2][:, :].rearrange("p (c n) -> p c n", n=P)
                    last = minus(htl[:, g % 2, 0:full, :], bank[:, 0:full, :], hth[:, g % 2, 0:full, :])
                    if full < len(CH[g]):
                        w = CH[g][full][1]
                        last = minus(htl[0:w, g % 2, full, :], bank[0:w, full, :], hth[0:w, g % 2, full, :])
                    last.then_inc(v_hl, 1)

                def add_to_x(t):
                    dve.wait_ge(t_dn, (t + 1) * NG)
                    V.scalar_tensor_tensor(x[:, t - t0, :], B[6][:, 0:HID], 0.5, x[:, t - t0, :], ALU.mult,
                                           ALU.add).then_inc(v_x, 1)

                link.at(linked[0])
                variance(t0)
                normalise(t0)
                low_x(t0, 0)
                negate_logits(t0)
                expert_weights(t0, 0)
                start = linked[0] + link.n
                per = link.n

                def tile(i, par, first, last):
                    t = i + t0
                    link.at(i * per + start)
                    for g in range(NG):
                        n = t * NG + g
                        if g == 0 and not last:
                            variance(t + 1)
                        middle(n, g, par, t)
                        if not (first and g == 0):
                            if g == 1 and not last:
                                low_x(t + 1, 1 - par)
                            low_hidden(n - 1, (g - 1) % NG)
                        if g == 0 and not last:
                            normalise(t + 1)
                        if g == 1 and not first:
                            add_to_x(t - 1)
                        if g == 2 and not last:
                            negate_logits(t + 1)
                        if g == 3 and not last:
                            expert_weights(t + 1, 1 - par)
                    assert last or link.n == per

                pairs(dve, 0, NT - 1, tile)
                low_hidden((t0 + NT) * NG - 1, NG - 1)
                add_to_x(t0 + NT - 1)
                linked[0] = start + (NT - 1) * per

            dve.wait_ge(a_wh, 1)
            minus(gate_l[:, :, :], gate_raw[:, :, :], gate_h[:, :, :]).then_inc(v_wl, 1)
            V.memset(mhalf[:, :], -0.5)
            V.memset(ebase[:, :], float(np.e)).then_inc(v_one, 1)
            for i in DVE_UNITS:
                kind, g = units[i]
                dve.wait_ge(a_wh, i + 2)
                src, hi, lo = unit_raw(i), unit_dst(i, 0), unit_dst(i, 1)
                full = sum(w == P for _, w in CH[g]) if kind == "d" else KH
                last = minus(lo[:, 0:full, :], src[:, 0:full, :], hi[:, 0:full, :])
                if kind == "d" and full < len(CH[g]):
                    w = CH[g][full][1]
                    last = minus(lo[0:w, full, :], src[0:w, full, :], hi[0:w, full, :])
                last.then_inc(v_wl, 1)
            dve.wait_ge(a_wh, len(units) + 2)
            minus(wqa_l[:, :, :], wqa_raw[:, :, :], wqa_h[:, :, :]).then_inc(v_wl, 1)
            dve.wait_ge(sp_x, 32)
            dve.wait_ge(sp_c, 8 * 16)

            ffn(0)

            link.at(linked[0])
            link(V.tensor_scalar(qs2[:, :], qs[:, :], SM_SCALE, None, ALU.mult))
            kvb = kvln_row[:, :].unsqueeze(1).broadcast_to([P, 8, KVL])
            for c in range(2):
                dve.wait_ge(t_w, c + 1)
                dve.wait_ge((sp_r1, sp_r2)[c], (16, 32)[c])
                if c:
                    dve.wait_ge(v_wlo, 1)
                for i in range(2):
                    V.scalar_tensor_tensor(wabs[:, 8 * i:8 * i + 8, 0:KVL],
                                           B[2 * c + i][:, :].rearrange("p (h n) -> p h n", h=8), qs2[:, c:c + 1],
                                           kvb, ALU.mult, ALU.mult)
                V.tensor_scalar(wabs[:, :, KVL:P], wabs[:, :, KVL:P], qs2[:, c:c + 1], None, ALU.mult).then_inc(v_w, 1)
                dve.wait_ge(a_w, c + 1)
                flat = wabs[:, :, :].rearrange("p h n -> p (h n)")
                if c == 0:
                    minus(wq1_l[:, :], flat, wq1_h[:, :]).then_inc(v_wlo, 1)
                else:
                    minus(wq2[64:P, :], flat[64:P, :], wq2[64:P, :]).then_inc(v_wlo, 1)
            dve.wait_ge(v_wlo, 2)
            V.memset(kvbv_raw[:, :, 64:128], 0.0).then_inc(v_pad, 1)
            dve.wait_ge(t_w, 3)
            for q in range(4):
                V.tensor_scalar(wvo_raw[:, 2 * q:2 * q + 2, :], B[4 + q][:, :].rearrange("p (r n) -> p r n", r=2),
                                kvln2[:, 0:1], None, ALU.mult).then_inc(v_w, 1)
            for q in range(4):
                dve.wait_ge(a_w, 3 + q)
                r = slice(2 * q, 2 * q + 2)
                minus(wvo_l[:, r, :], wvo_raw[:, r, :], wvo_h[:, r, :]).then_inc(v_wlo, 1)
            dve.wait_ge(v_wlo, 6)
            linked[0] += link.n

            def attention():
                def variances(b):
                    for j in range(2):
                        V.bn_stats(ast6[:, j, :], x[:, TPS * b + j, :]).then_inc(v_link, 1)
                    link.n += 2
                    dve.wait_ge(v_link, link.base + link.n)
                    dve.sem_inc(v_turn, 1)
                    for j in range(2):
                        V.bn_aggr(amv[:, j, :], ast6[:, j, :]).then_inc(v_link, 1)
                    link.n += 2
                    dve.wait_ge(v_link, link.base + link.n)
                    V.tensor_scalar(ave[:, :], amv[:, :, 1], LN_EPS, None, ALU.add).then_inc(v_ast, 1)

                def normalise(b):
                    dve.wait_ge(g_ars, b + 1)
                    for j in range(2):
                        last = V.tensor_scalar(xn[:, j, :], x[:, TPS * b + j, :], amv[:, j, 0:1], arstd[:, j:j + 1],
                                               ALU.subtract, ALU.mult)
                    last.then_inc(v_axn, 1)

                def low_x(b):
                    for j in range(2):
                        dve.wait_ge(a_ax, 2 * b + j + 1)
                        minus(xl[j][:, :, :], B[6 + j][:, 0:HID].rearrange("p (k n) -> p k n", k=KH),
                              xh[j][:, :, :]).then_inc(v_ax, 1)

                def squares_eps(b):
                    dve.wait_ge(a_ms, b + 1)
                    V.tensor_scalar(mse[:, :, :], ms[:, :, :], RMS_EPS, None, ALU.add).then_inc(v_ms, 1)

                def latents(b, par):
                    dve.wait_ge(g_rr, b + 1)
                    half = DR // 2
                    kpe = qa[:, :, QLR + KVL:QA]
                    V.tensor_tensor(kr[:, :, 0, :], kpe, cos[:, :, :], ALU.mult)
                    V.tensor_tensor(kr[:, :, 1, 0:half], kpe[:, :, half:DR], sin[:, :, 0:half], ALU.mult)
                    link(V.tensor_tensor(kr[:, :, 1, half:DR], kpe[:, :, 0:half], sin[:, :, half:DR], ALU.mult))
                    for j in range(2):
                        r0, r1 = rr[:, j, 0:1], rr[:, j, 1:2]
                        flat = cq[:, j, :, :].rearrange("p k n -> p (k n)")
                        V.tensor_scalar(flat[:, 0:QLR], qa[:, j, 0:QLR], r0, None, ALU.mult)
                        V.tensor_scalar(flat[:, QLR:2 * P], qa[:, j, P:QLR], r0, None, ALU.mult)
                        V.tensor_scalar(flat[:, 2 * P:2 * P + KVL], qa[:, j, QLR:QLR + KVL], r1, None, ALU.mult)
                        V.tensor_scalar(vpad[par][j][:, KVL:2 * KVL], qa[:, j, QLR:QLR + KVL], r1, None, ALU.mult)
                    V.tensor_tensor(cq[:, :, 2, KVL:P], kr[:, :, 0, :], kr[:, :, 1, :], ALU.add).then_inc(v_cq, 1)

                def low_latents(b, par):
                    for j in range(2):
                        dve.wait_ge(a_at, 2 * b + j + 1)
                        minus(tl[par][:, :, j, :], B[6 + j][:, 0:3 * P].rearrange("p (k n) -> p k n", k=3),
                              th[par][:, :, j, :]).then_inc(v_at, 1)

                def rotate_queries(c):
                    half = DR // 2
                    for j in range(2):
                        dve.wait_ge(t_q, 2 * c + j + 1)
                        dve.wait_ge(a_q, 2 * c + j + 1)
                        pe_part = B[6 + j][:, :].rearrange("p (h n) -> p h n", h=HG)[:, :, KVL:P]

                        def table(tab, a, w):
                            return tab[:, j, a:a + w].unsqueeze(1).broadcast_to([P, HG, w])

                        V.tensor_tensor(qsb[:, j, :, KVL:P], pe_part, table(cos, 0, DR), ALU.mult)
                        V.tensor_tensor(rt2[:, j, :, 0:half], pe_part[:, :, half:DR], table(sin, 0, half), ALU.mult)
                        V.tensor_tensor(rt2[:, j, :, half:DR], pe_part[:, :, 0:half], table(sin, half, half),
                                        ALU.mult).then_inc(v_q, 1)

                def low_queries(c, gi):
                    for j in range(2):
                        dve.wait_ge(a_qt, 2 * c + j + 1)
                        minus(qtl[:, j, :, :], B[6 + j][:, :].rearrange("p (h n) -> p h n", h=HG),
                              qth[:, j, :, :]).then_inc(v_qt, 1)

                def maxima(c, gi, u):
                    m, k = 3 * c + u, unit_par(gi, u)
                    dve.wait_ge(t_s, m + 1)
                    nh = 4 if u == 0 else 2
                    s_ = B[k][:, :].rearrange("p (h n) -> p h n", h=nh)
                    diag = s_ if u == 0 else s_[:, :, P:SEQ]
                    link(V.tensor_tensor(diag, diag, mask[:, :].unsqueeze(1).broadcast_to([P, nh, P]), ALU.add))
                    V.tensor_reduce(nmax[:, k, 0:nh], s_, AX.X, ALU.max, negate=True).then_inc(v_m, 1)

                def reciprocals(c, gi, u):
                    m, k = 3 * c + u, unit_par(gi, u)
                    dve.wait_ge(a_e, m + 1)
                    nh = 4 if u == 0 else 2
                    V.reciprocal(rcp[:, u, 0:nh], rsum[:, u, 0:nh]).then_inc(v_r, 1)

                def low_outputs(c, gi):
                    dve.wait_ge(a_o, c + 1)
                    minus(otl[gi % 2][:, :, :], B[4][:, :].rearrange("p (r q) -> p r q", r=2),
                          oth[gi % 2][:, :, :]).then_inc(v_o, 1)

                def add_to_x(b):
                    dve.wait_ge(t_p, NHG * b + NHG)
                    V.tensor_tensor(x[:, bass.ds(TPS * b, TPS), :], B[5][:, :].rearrange("p (j n) -> p j n", j=TPS),
                                    x[:, bass.ds(TPS * b, TPS), :], ALU.add).then_inc(v_ux, 1)

                link.at(linked[0])
                for i in range(2):
                    for j in range(2):
                        V.memset(vpad[i][j][:, 0:KVL], 0.0)
                        V.memset(vpad[i][j][:, 2 * KVL:3 * KVL], 0.0)
                variances(0)
                normalise(0)
                low_x(0)
                squares_eps(0)
                latents(0, 0)
                low_latents(0, 0)
                rotate_queries(0)
                low_queries(0, 0)
                start = linked[0] + link.n
                per = 5 + 3 * NHG

                def sequence(b, par, first, last):
                    link.at(b * per + start)
                    for gi in range(NHG):
                        c = NHG * b + gi
                        end = last and gi == NHG - 1
                        if not last:
                            if gi == 0:
                                variances(b + 1)
                            if gi == 1:
                                low_x(b + 1)
                            if gi == 3:
                                low_latents(b + 1, 1 - par)
                        maxima(c, gi, 0)
                        if not end:
                            rotate_queries(c + 1)
                        reciprocals(c, gi, 0)
                        maxima(c, gi, 1)
                        maxima(c, gi, 2)
                        reciprocals(c, gi, 1)
                        if gi == 2 and not last:
                            squares_eps(b + 1)
                        reciprocals(c, gi, 2)
                        if not (first and gi == 0):
                            low_outputs(c - 1, (gi - 1) % NHG)
                        if not end:
                            low_queries(c + 1, (gi + 1) % NHG)
                        if gi == 0 and not last:
                            normalise(b + 1)
                        if gi == 2 and not last:
                            latents(b + 1, 1 - par)
                        if gi == 1 and not first:
                            add_to_x(b - 1)
                    assert last or link.n == per, link.n

                pairs(dve, 0, NSEQ - 1, sequence)
                low_outputs(NHG * NSEQ - 1, NHG - 1)
                add_to_x(NSEQ - 1)
                linked[0] = start + (NSEQ - 1) * per + link.n

            attention()
            dve.wait_ge(v_ux, NSEQ)
            ffn(1)

        @block.gpsimd
        def _(pool):
            G = nc.gpsimd

            def ffn(f):
                t0 = NT * f

                def rstd_of(t):
                    pool.wait_ge(v_st, t + 1)
                    G.tensor_tensor(rstd[:, :], ve[:, :], mhalf[:, 0:1], ALU.pow).then_inc(g_rs, 1)

                def exp_of(t):
                    pool.wait_ge(v_nl, t + 1)
                    G.tensor_tensor(en[:, :], ebase[:, :], nl[:, :], ALU.pow).then_inc(g_en, 1)

                rstd_of(t0)
                exp_of(t0)

                def tile(i, par, first, last):
                    if not last:
                        rstd_of(i + t0 + 1)
                        exp_of(i + t0 + 1)

                pairs(pool, 0, NT - 1, tile)

            pool.wait_ge(v_one, 1)
            for i in POOL_UNITS:
                pool.wait_ge(a_wh, i + 2)
                G.tensor_tensor(unit_dst(i, 1), unit_raw(i), unit_dst(i, 0).bitcast(F32), ALU.subtract).then_inc(g_wl, 1)
            ffn(0)

            def attention():
                def rstd_of(b):
                    pool.wait_ge(v_ast, b + 1)
                    G.tensor_tensor(arstd[:, :], ave[:, :], mhalf[:, 0:2], ALU.pow).then_inc(g_ars, 1)

                def rms_of(b):
                    pool.wait_ge(v_ms, b + 1)
                    G.tensor_tensor(rr[:, :, :].rearrange("p j i -> p (j i)"), mse[:, :, :].rearrange("p j i -> p (j i)"),
                                    mhalf[:, 0:4], ALU.pow).then_inc(g_rr, 1)

                def add_rotation(c):
                    for j in range(2):
                        pool.wait_ge(v_q, 2 * c + j + 1)
                        G.tensor_tensor(qsb[:, j, :, KVL:P], qsb[:, j, :, KVL:P], rt2[:, j, :, :], ALU.add).then_inc(g_q, 1)

                def probabilities(c, gi, u):
                    m, k = 3 * c + u, unit_par(gi, u)
                    pool.wait_ge(v_r, m + 1)
                    nh = 4 if u == 0 else 2
                    w = 512 // nh
                    place = prob[:, u, :].rearrange("p (h n) -> p h n", h=nh)
                    G.tensor_tensor(place, place, rcp[:, u, 0:nh].unsqueeze(2).broadcast_to([P, nh, w]), ALU.mult).then_inc(g_n, 1)

                rstd_of(0)
                rms_of(0)
                add_rotation(0)

                def sequence(b, par, first, last):
                    for gi in range(NHG):
                        c = NHG * b + gi
                        if gi == 0 and not last:
                            rstd_of(b + 1)
                        if not (last and gi == NHG - 1):
                            add_rotation(c + 1)
                        probabilities(c, gi, 0)
                        probabilities(c, gi, 1)
                        if gi == 2 and not last:
                            rms_of(b + 1)
                        probabilities(c, gi, 2)

                pairs(pool, 0, NSEQ - 1, sequence)

            attention()
            ffn(1)


def kernel(**inputs):
    import concourse.bacc as bacc
    from concourse.bass_utils import run_bass_kernel_spmd

    a = {k.replace("L0_", ""): np.asarray(v) for k, v in inputs.items()}
    qb = a["attn_w_qb"].reshape(NH, DN + DR, QLR)
    kvb = a["attn_w_kvb"].reshape(NH, DN + DV, KVL)
    qln, kvln = a["attn_q_a_ln_w"], a["attn_kv_a_ln_w"]
    inv = (np.float32(1.0) / np.float32(10000.0) ** (np.arange(0, DR, 2, dtype=np.float32) / np.float32(DR))).astype(np.float32)
    ang = np.outer(np.arange(SEQ, dtype=np.float32), inv).astype(np.float32)
    cos, sin = np.cos(ang), np.sin(ang)

    def tiles(t):
        return t.reshape(TPS, P, DR).transpose(1, 0, 2)

    arrays = {
        "x": a["attn_hidden_states"],
        "gate": a["ffn_gate_w"].T,
        "wg": np.concatenate([a["ffn_exp_wg"].reshape(NE * EFF, HID), a["ffn_shared_wg"]]).T,
        "wu": np.concatenate([a["ffn_exp_wu"].reshape(NE * EFF, HID), a["ffn_shared_wu"]]).T,
        "wd": np.concatenate([a["ffn_exp_wd"].transpose(0, 2, 1).reshape(NE * EFF, HID), a["ffn_shared_wd"].T]),
        "wqa": np.concatenate([a["attn_w_qa"], a["attn_w_kva"]]).T,
        "wqbn": qb[:, :DN].transpose(1, 0, 2),
        "wqbp": qb[:, DN:].transpose(2, 0, 1),
        "kvbk": kvb[:, :DN].transpose(1, 0, 2),
        "kvbv": kvb[:, DN:].transpose(1, 0, 2),
        "wo": a["attn_w_o"].reshape(HID, NH, DV).transpose(2, 1, 0),
        "qln": np.stack([qln[0:P], np.concatenate([qln[P:QLR], qln[P:QLR]])], axis=1),
        "kvln2": np.concatenate([kvln, kvln])[:, None],
        "kvln_row": np.repeat(kvln[None, :], P, axis=0),
        "ident": np.eye(P, dtype=np.float32),
        "mask": np.where(np.arange(P)[None, :] <= np.arange(P)[:, None], 0.0, -1e30).astype(np.float32),
        "tri8": np.repeat(np.tri(NE, NE, -1, dtype=np.float32)[None], P, axis=0),
        "cos": tiles(np.concatenate([cos, cos], axis=1)),
        "sin": tiles(np.concatenate([-sin, sin], axis=1)),
    }
    arrays = {k: np.ascontiguousarray(v) for k, v in arrays.items()}
    nc = bacc.Bacc("TRN2", target_bir_lowering=False, num_devices=1, dynamic_dma_scratch_size=8192)
    d = {k: nc.dram_tensor("in_" + k, v.shape, F32, kind="ExternalInput").ap() for k, v in arrays.items()}
    out = nc.dram_tensor("out", arrays["x"].shape, F32, kind="ExternalOutput").ap()
    build(nc, d, out)
    r = run_bass_kernel_spmd(nc, [{"in_" + k: v for k, v in arrays.items()}], core_ids=[0])
    return r.results[0]["out"]
```

```python
from contextlib import ExitStack

import numpy as np

import concourse.bass as bass
from concourse import mybir

F32 = mybir.dt.float32
F32R = mybir.dt.float32r
ALU = mybir.AluOpType
ACT = mybir.ActivationFunctionType
AX = mybir.AxisListType

P = 128
HID = 256
KH = HID // P
NSEQ, SEQ = 8, 256
TPS = SEQ // P
NT = NSEQ * TPS
NE, EFF, SFF = 8, 176, 352
FF = NE * EFF + SFF
GW = 512
NG = -(-FF // GW)
GWID = [min(GW, FF - GW * g) for g in range(NG)]
CH = [[(c, min(P, GWID[g] - c)) for c in range(0, GWID[g], P)] for g in range(NG)]
NCH = sum(len(c) for c in CH)
TOPK_SCALE = 2.5
NH, QLR, KVL, DN, DR, DV = 16, 192, 64, 128, 64, 128
HG = 4
NHG = NH // HG
NUNIT = 3
SM_SCALE = float(DN + DR) ** -0.5
LN_EPS, RMS_EPS = 1e-5, 1e-6
QA = QLR + KVL + DR


class Link:

    def __init__(self, eng, sem):
        self.eng, self.sem, self.base, self.n = eng, sem, 0, 0

    def at(self, base):
        self.base, self.n = base, 0

    def __call__(self, ins):
        self.n += 1
        ins.then_inc(self.sem, 1)
        self.eng.wait_ge(self.sem, self.base + self.n)


def build(nc, d, out):
    with ExitStack() as ctx:
        def sb(name, shape, dt=F32, c=ctx):
            return c.enter_context(nc.sbuf_tensor(name, shape, dt))

        def sem(name):
            return ctx.enter_context(nc.semaphore(name))

        x = sb("x", [P, NT, HID])
        wg_h = sb("wg_h", [P, KH, FF], F32R)
        wg_l = sb("wg_l", [P, KH, FF], F32R)
        wu_h = sb("wu_h", [P, KH, FF], F32R)
        wu_l = sb("wu_l", [P, KH, FF], F32R)
        wd_h = sb("wd_h", [P, NCH, HID], F32R)
        wd_l = sb("wd_l", [P, NCH, HID], F32R)
        gate_h = sb("gate_h", [P, KH, NE], F32R)
        gate_l = sb("gate_l", [P, KH, NE], F32R)
        wq1_h = sb("wq1_h", [P, NH * P], F32R)
        wq1_l = sb("wq1_l", [P, NH * P], F32R)
        wq2 = sb("wq2", [P, NH * P], F32R)
        wvo_h = sb("wvo_h", [P, NH // 2, HID], F32R)
        wvo_l = sb("wvo_l", [P, NH // 2, HID], F32R)
        wqa_h = sb("wqa_h", [P, KH, QA], F32R)
        wqa_l = sb("wqa_l", [P, KH, QA], F32R)
        ident = sb("ident", [P, P])
        mask = sb("mask", [P, P])
        tri8 = sb("tri8", [P, NE, NE])
        cos = sb("cos", [P, TPS, DR])
        sin = sb("sin", [P, TPS, DR])
        kvln_row = sb("kvln_row", [P, KVL])
        kvln2 = sb("kvln2", [P, 1])
        qs = sb("qs", [P, 2])
        mhalf = sb("mhalf", [P, 4])
        ebase = sb("ebase", [P, NE])
        gate_raw = sb("gate_raw", [P, KH, NE])
        qs2 = sb("qs2", [P, 2])
        st6 = sb("st6", [P, 6])
        mv = sb("mv", [P, 2])
        ve = sb("ve", [P, 1])
        rstd = sb("rstd", [P, 1])
        xn = sb("xn", [P, 2, HID])

        xh = [sb(f"xh{i}", [P, KH, P], F32R) for i in range(2)]
        xl = [sb(f"xl{i}", [P, KH, P], F32R) for i in range(2)]
        low = ExitStack()
        silu = sb("silu", [P, 2, GW], c=low)
        hid = sb("hid", [P, 2, GW], c=low)
        hth = sb("hth", [P, 2, 4, P], F32R, c=low)
        htl = sb("htl", [P, 2, 4, P], F32R, c=low)
        nl = sb("nl", [P, NE], c=low)
        en = sb("en", [P, NE], c=low)
        en1 = sb("en1", [P, NE], c=low)
        sg = sb("sg", [P, NE], c=low)
        cgt = sb("cgt", [P, NE, NE], c=low)
        cge = sb("cge", [P, NE, NE], c=low)
        cgl = sb("cgl", [P, NE, NE], c=low)
        cbt = sb("cbt", [P, NE, NE], c=low)
        cnt = sb("cnt", [P, NE], c=low)
        msk = sb("msk", [P, NE], c=low)
        den = sb("den", [P, 3], c=low)
        wgt = sb("wgt", [P, 2, NE], c=low)
        stage = ExitStack()
        NRING = 8
        ring = sb("ring", [P, NRING, 1024], c=stage)
        wqa_raw = sb("wqa_raw", [P, KH, QA], c=stage)
        stage.close()
        stage = ExitStack()
        wqb_raw = sb("wqb_raw", [P, NH, 2 * P], c=stage)
        rot1_raw = sb("rot1_raw", [P, NH, DR], c=stage)
        rot2_raw = sb("rot2_raw", [P, NH, DR], c=stage)
        kvbk_raw = sb("kvbk_raw", [P, NH, KVL], c=stage)
        kvbv_raw = sb("kvbv_raw", [P, NH // 2, 192], c=stage)
        wo_raw = sb("wo_raw", [P, NH, HID], c=stage)
        stage.close()
        low.close()

        qa = sb("qa", [P, 2, QA])
        cq = sb("cq", [P, 2, 3, P])
        kr = sb("kr", [P, 2, 2, DR])
        ast6 = sb("ast6", [P, 2, 6])
        amv = sb("amv", [P, 2, 2])
        ave = sb("ave", [P, 2])
        arstd = sb("arstd", [P, 2])
        ms = sb("ms", [P, 2, 2])
        mse = sb("mse", [P, 2, 2])
        rr = sb("rr", [P, 2, 2])
        nmax = sb("nmax", [P, NUNIT, HG])
        rsum = sb("rsum", [P, NUNIT, HG])
        rcp = sb("rcp", [P, NUNIT, HG])
        vpad = [[sb(f"vpad{i}{j}", [P, 192]) for j in range(2)] for i in range(2)]
        qsb = sb("qsb", [P, 2, HG, P])
        th = [sb(f"th{i}", [P, 3, 2, P], F32R) for i in range(2)]
        tl = [sb(f"tl{i}", [P, 3, 2, P], F32R) for i in range(2)]
        rt2 = sb("rt2", [P, 2, HG, DR])
        qth = sb("qth", [P, 2, HG, P], F32R)
        qtl = sb("qtl", [P, 2, HG, P], F32R)
        prob = sb("prob", [P, NUNIT, 512])
        pt0 = sb("pt0", [P, HG, SEQ])
        pt1 = sb("pt1", [P, HG, P])
        oth = [sb(f"oth{i}", [P, 2, SEQ], F32R) for i in range(2)]
        otl = [sb(f"otl{i}", [P, 2, SEQ], F32R) for i in range(2)]

        B = [ctx.enter_context(nc.psum_tensor(f"B{i}", [P, 512], F32)) for i in range(8)]

        sp_x0 = sem("sp_x0")
        sp_x = sem("sp_x")
        sp_c = sem("sp_c")
        sp_c2 = sem("sp_c2")
        sp_w = [sem(f"sp_w{i}") for i in range(12)]
        sp_gate = sem("sp_gate")
        sp_qa = sem("sp_qa")
        sp_a1 = sem("sp_a1")
        sp_a2 = sem("sp_a2")
        sp_out = sem("sp_out")
        a_wh = sem("a_wh")
        v_wl = sem("v_wl")
        g_wl = sem("g_wl")
        v_one = sem("v_one")
        v_link = sem("v_link")
        v_turn = sem("v_turn")
        v_st = sem("v_st")
        g_rs = sem("g_rs")
        v_xn = sem("v_xn")
        t_xt = sem("t_xt")
        a_xh = sem("a_xh")
        v_xl = sem("v_xl")
        t_lg = sem("t_lg")
        v_nl = sem("v_nl")
        g_en = sem("g_en")
        v_wt = sem("v_wt")
        t_g = sem("t_g")
        t_u = sem("t_u")
        a_sl = sem("a_sl")
        v_h = sem("v_h")
        t_ht = sem("t_ht")
        a_hh = sem("a_hh")
        v_hl = sem("v_hl")
        t_dn = sem("t_dn")
        v_x = sem("v_x")
        v_pad = sem("v_pad")
        t_w = sem("t_w")
        a_w = sem("a_w")
        v_aw = sem("v_aw")
        v_ast = sem("v_ast")
        g_ars = sem("g_ars")
        v_axn = sem("v_axn")
        t_ax = sem("t_ax")
        a_ax = sem("a_ax")
        v_ax = sem("v_ax")
        t_qa = sem("t_qa")
        a_qa = sem("a_qa")
        a_ms = sem("a_ms")
        v_ms = sem("v_ms")
        g_rr = sem("g_rr")
        v_cq = sem("v_cq")
        t_at = sem("t_at")
        a_at = sem("a_at")
        v_at = sem("v_at")
        t_q = sem("t_q")
        a_q = sem("a_q")
        v_q = sem("v_q")
        g_q = sem("g_q")
        t_qt = sem("t_qt")
        a_qt = sem("a_qt")
        v_qt = sem("v_qt")
        t_s = sem("t_s")
        v_m = sem("v_m")
        a_e = sem("a_e")
        v_r = sem("v_r")
        g_n = sem("g_n")
        t_t = sem("t_t")
        a_t = sem("a_t")
        t_o = sem("t_o")
        a_o = sem("a_o")
        v_o = sem("v_o")
        t_p = sem("t_p")
        v_ux = sem("v_ux")

        units = []
        for g in range(NG):
            units += [("g", g), ("u", g)]
            if g >= 1:
                units.append(("d", g - 1))
        units.append(("d", NG - 1))
        uidx = {u: i for i, u in enumerate(units)}
        WCUT = [4, 7, 9, 11, 12]

        def unit_raw(i):
            kind, g = units[i]
            r = ring[:, i % NRING, :]
            if kind == "d":
                n = len(CH[g])
                return r[:, 0:n * HID].rearrange("p (c n) -> p c n", c=n)
            return r[:, 0:KH * GWID[g]].rearrange("p (k n) -> p k n", k=KH)

        def unit_dst(i, lo):
            kind, g = units[i]
            if kind == "d":
                return (wd_l if lo else wd_h)[:, 4 * g:4 * g + len(CH[g]), :]
            w = {"g": (wg_h, wg_l), "u": (wu_h, wu_l)}[kind][lo]
            return w[:, :, GW * g:GW * g + GWID[g]]

        def lo_on_pool(i):
            return units[i][0] == "u"

        DVE_UNITS = [i for i in range(12) if not lo_on_pool(i)]
        POOL_UNITS = [i for i in range(12) if lo_on_pool(i)]

        def wait_unit(eng, key):
            i = uidx[key]
            if lo_on_pool(i):
                eng.wait_ge(g_wl, POOL_UNITS.index(i) + 1)
            else:
                eng.wait_ge(v_wl, DVE_UNITS.index(i) + 2)

        def segments(g):
            lo, hi = GW * g, GW * g + GWID[g]
            segs = [(e * EFF, (e + 1) * EFF, e) for e in range(NE)] + [(NE * EFF, FF, None)]
            return [(max(a, lo) - lo, min(b, hi) - max(a, lo), e) for a, b, e in segs if a < hi and b > lo]

        PROB_BANK = (3, 4, 3)

        def split3(mm, out_, lh, ll, rh, rl, start, stop, **kw):
            mm(out_, lh, rh, start=start, stop=False, **kw)
            mm(out_, lh, rl, start=False, stop=False, **kw)
            return mm(out_, ll, rh, start=False, stop=stop, **kw)

        block = ctx.enter_context(nc.Block())
        out_v = out.rearrange("b (h p) d -> p (b h) d", p=P)
        x_v = d["x"].rearrange("b (h p) d -> p (b h) d", p=P)

        def pairs(eng, first, last, body):
            body(first, first % 2, True, False)
            with eng.Fori(first + 1, last - 1, 2) as i:
                body(i, (first + 1) % 2, False, False)
                body(i + 1, first % 2, False, False)
            body(last, last % 2, False, True)

        @block.sync
        def _(sp):
            sp.dma_start(x[:, 0:2, :], x_v[:, 0:2, :]).then_inc(sp_x0, 16)
            sp.dma_start(gate_raw[:, :, :], d["gate"].rearrange("(k p) n -> p k n", p=P)).then_inc(sp_gate, 16)
            for t_, s_ in ((ident, "ident"), (tri8, "tri8")):
                sp.dma_start(t_[tuple(slice(None) for _ in t_.shape)], d[s_]).then_inc(sp_c, 16)

            def load_unit(i):
                kind, g = units[i]
                if i >= NRING:
                    wait_unit(sp, units[i - NRING])
                if kind == "d":
                    n = sum(w == P for _, w in CH[g])
                    src = d["wd"][GW * g:GW * g + n * P, :].rearrange("(c p) n -> p c n", p=P)
                    sp.dma_start(unit_raw(i)[:, 0:n, :], src).then_inc(sp_w[i], 16)
                    if n < len(CH[g]):
                        w = CH[g][n][1]
                        sp.dma_start(unit_raw(i)[0:w, n, :], d["wd"][GW * g + n * P:FF, :]).then_inc(sp_w[i], 16)
                else:
                    src = d["w" + kind].rearrange("(k p) n -> p k n", p=P)[:, :, GW * g:GW * g + GWID[g]]
                    sp.dma_start(unit_raw(i), src).then_inc(sp_w[i], 16)

            for i in range(4):
                load_unit(i)
            sp.dma_start(x[:, 2:8, :], x_v[:, 2:8, :]).then_inc(sp_x, 16)
            for i in range(4, 12):
                load_unit(i)
            sp.dma_start(x[:, 8:NT, :], x_v[:, 8:NT, :]).then_inc(sp_x, 16)
            sp.dma_start(wqa_raw[:, :, :], d["wqa"].rearrange("(k p) n -> p k n", p=P)).then_inc(sp_qa, 16)
            for t_, s_ in ((mask, "mask"), (cos, "cos"), (sin, "sin"), (kvln_row, "kvln_row"), (kvln2, "kvln2"),
                           (qs, "qln")):
                sp.dma_start(t_[tuple(slice(None) for _ in t_.shape)], d[s_]).then_inc(sp_c2, 16)
            sp.wait_ge(v_wl, len(DVE_UNITS) + 2)
            sp.wait_ge(g_wl, len(POOL_UNITS))
            sp.dma_start(wqb_raw[:, :, 0:QLR], d["wqbn"]).then_inc(sp_a1, 16)
            sp.dma_start(wqb_raw[:, :, QLR:2 * P], d["wqbn"][:, :, P:QLR]).then_inc(sp_a1, 16)
            sp.dma_start(kvbk_raw[:, :, :], d["kvbk"]).then_inc(sp_a1, 16)
            sp.dma_start(rot1_raw[:, :, :], d["wqbp"][0:P]).then_inc(sp_a1, 16)
            for i in range(2):
                sp.dma_start(rot2_raw[64 * i:64 * i + 64, :, :], d["wqbp"][P:QLR]).then_inc(sp_a1, 16)
            kv = d["kvbv"].rearrange("p (h e) n -> p h e n", e=2)
            sp.dma_start(kvbv_raw[:, :, 0:64], kv[:, :, 0, :]).then_inc(sp_a2, 16)
            sp.dma_start(kvbv_raw[:, :, 128:192], kv[:, :, 1, :]).then_inc(sp_a2, 16)
            sp.dma_start(wo_raw[:, :, :], d["wo"]).then_inc(sp_a2, 16)
            done = 0
            for n in (6, 6, 3, 1):
                sp.wait_ge(v_x, NT + done + n)
                sp.dma_start(out_v[:, done:done + n, :], x[:, done:done + n, :]).then_inc(sp_out, 16)
                done += n
            sp.wait_ge(sp_out, 64)

        @block.tensor
        def _(pe):
            mm, tr = nc.tensor.matmul, nc.tensor.transpose

            def ffn(f):
                t0 = NT * f

                def xt(t):
                    pe.wait_ge(v_xn, t + 1)
                    if not (isinstance(t, int) and t == 0):
                        pe.wait_ge(v_nl, t)
                    for k in range(KH):
                        last = tr(B[7][:, k * P:(k + 1) * P], xn[:, 0, k * P:(k + 1) * P], ident[:, :])
                    last.then_inc(t_xt, 1)

                def logits(t, par):
                    pe.wait_ge(v_xl, t + 1)
                    for k in range(KH):
                        last = split3(mm, B[7][:, 256:256 + NE], xh[par][:, k, :], xl[par][:, k, :],
                                      gate_h[:, k, :], gate_l[:, k, :], k == 0, k == KH - 1)
                    last.then_inc(t_lg, 1)

                def up(n, g, par):
                    if not (isinstance(n, int) and n < 2):
                        pe.wait_ge(v_h, n - 1)
                    for w_h, w_l, bank, kind, s_ in ((wg_h, wg_l, B[g % 2], "g", t_g), (wu_h, wu_l, B[2 + g % 2], "u", t_u)):
                        if isinstance(n, int) and n < NG:
                            wait_unit(pe, (kind, g))
                        c = slice(GW * g, GW * g + GWID[g])
                        for k in range(KH):
                            last = split3(mm, bank[:, 0:GWID[g]], xh[par][:, k, :], xl[par][:, k, :],
                                          w_h[:, k, c], w_l[:, k, c], k == 0, k == KH - 1)
                        last.then_inc(s_, 1)

                def ht(n, g):
                    pe.wait_ge(v_h, n + 1)
                    if not (isinstance(n, int) and n < 2):
                        pe.wait_ge(v_hl, n - 1)
                    for i, (c, w) in enumerate(CH[g]):
                        last = tr(B[4 + g % 2][0:w, i * P:(i + 1) * P], hid[:, g % 2, c:c + w], ident[:, :])
                    last.then_inc(t_ht, 1)

                def down(n, g, t):
                    pe.wait_ge(v_hl, n + 1)
                    if isinstance(n, int) and n < NG:
                        wait_unit(pe, ("d", g))
                    if g == 0 and not (isinstance(t, int) and t == 0):
                        pe.wait_ge(v_x, t)
                    for i, (c, w) in enumerate(CH[g]):
                        last = split3(mm, B[6][:, 0:HID], hth[0:w, g % 2, i, :], htl[0:w, g % 2, i, :],
                                      wd_h[0:w, 4 * g + i, :], wd_l[0:w, 4 * g + i, :],
                                      g == 0 and i == 0, g == NG - 1 and i == len(CH[g]) - 1)
                    last.then_inc(t_dn, 1)

                if f == 0:
                    pe.wait_ge(sp_c, 2 * 16)
                    pe.wait_ge(v_wl, 1)
                else:
                    pe.wait_ge(v_ux, NSEQ)
                xt(t0)
                logits(t0, 0)

                def tile(i, par, first, last):
                    t = i + t0
                    n = t * NG
                    for g in range(NG):
                        up(n + g, g, par)
                        if g == 1 and not last:
                            xt(t + 1)
                        if g == 2 and not last:
                            logits(t + 1, 1 - par)
                        if not (first and g == 0):
                            ht(n + g - 1, (g - 1) % NG)
                        if not (first and g < 2):
                            down(n + g - 2, (g - 2) % NG, t if g >= 2 else t - 1)

                pairs(pe, 0, NT - 1, tile)
                n = (t0 + NT) * NG
                ht(n - 1, NG - 1)
                down(n - 2, NG - 2, t0 + NT - 1)
                down(n - 1, NG - 1, t0 + NT - 1)

            def query_weights(c):
                for h in range(NH):
                    last = mm(B[2 * c + h // 8][:, (h % 8) * KVL:(h % 8 + 1) * KVL],
                              wqb_raw[:, h, c * P:(c + 1) * P], kvbk_raw[:, h, :], start=True, stop=True)
                    if h % 8 == 7:
                        last.then_inc(t_w, 1)

            def output_weights():
                for q, bank in enumerate((4, 5, 0, 1)):
                    if q >= 2:
                        pe.wait_ge(v_aw, q - 1)
                    for p in range(2 * q, 2 * q + 2):
                        for e in range(2):
                            last = mm(B[bank][:, (p % 2) * HID:(p % 2 + 1) * HID], kvbv_raw[:, p, 64 * e:64 * e + P],
                                      wo_raw[:, 2 * p + e, :], start=(e == 0), stop=(e == 1))
                    last.then_inc(t_w, 1)

            def attention():
                def transpose_x(b):
                    pe.wait_ge(v_axn, b + 1)
                    for j in range(2):
                        for k in range(KH):
                            last = tr(B[6 + j][:, k * P:(k + 1) * P], xn[:, j, k * P:(k + 1) * P], ident[:, :])
                        last.then_inc(t_ax, 1)

                def down_projections(b):
                    for j in range(2):
                        pe.wait_ge(v_ax, 2 * b + j + 1)
                        for k in range(KH):
                            last = split3(mm, B[6 + j][:, 0:QA], xh[j][:, k, :], xl[j][:, k, :],
                                          wqa_h[:, k, :], wqa_l[:, k, :], k == 0, k == KH - 1)
                        last.then_inc(t_qa, 1)

                def transpose_latents(b):
                    pe.wait_ge(v_cq, b + 1)
                    for j in range(2):
                        for k in range(3):
                            last = tr(B[6 + j][:, k * P:(k + 1) * P], cq[:, j, k, :], ident[:, :])
                        last.then_inc(t_at, 1)

                def queries(gi, par, j):
                    cs = slice(512 * gi, 512 * gi + 512)
                    split3(mm, B[6 + j][:, :], th[par][:, 0, j, :], tl[par][:, 0, j, :], wq1_h[:, cs], wq1_l[:, cs],
                           True, False)
                    mm(B[6 + j][:, :], th[par][:, 1, j, :], wq2[:, cs], start=False, stop=False)
                    mm(B[6 + j][:, :], tl[par][:, 1, j, :], wq2[:, cs], start=False, stop=True).then_inc(t_q, 1)

                def transpose_queries(c, j):
                    pe.wait_ge(a_q, 2 * c + j + 1)
                    pe.wait_ge(g_q, 2 * c + j + 1)
                    for h in range(HG):
                        last = tr(B[6 + j][:, h * P:(h + 1) * P], qsb[:, j, h, :], ident[:, :])
                    last.then_inc(t_qt, 1)

                def scores(c, u, par):
                    j, heads, nk = (0, range(4), 1) if u == 0 else (1, range(2 * u - 2, 2 * u), 2)
                    pe.wait_ge(v_qt, 2 * c + j + 1)
                    if not (isinstance(c, int) and c == 0):
                        pe.wait_ge(a_e, 3 * c - 2 + u)
                    for i, h in enumerate(heads):
                        last = split3(mm, B[u][:, i * nk * P:(i + 1) * nk * P], qth[:, j, h, :], qtl[:, j, h, :],
                                      th[par][:, 2, 0:nk, :], tl[par][:, 2, 0:nk, :], True, True)
                    last.then_inc(t_s, 1)

                def transpose_probs(c, u):
                    pe.wait_ge(g_n, 3 * c + u + 1)
                    if u == 2:
                        pe.wait_ge(a_t, 3 * c + 1)
                    elif u == 0 and not (isinstance(c, int) and c == 0):
                        pe.wait_ge(a_t, 3 * c)
                    for i in range(4):
                        src = i if u == 0 else 2 * (i % 2) + i // 2
                        last = tr(B[PROB_BANK[u]][:, i * P:(i + 1) * P], prob[:, u, src * P:(src + 1) * P], ident[:, :])
                    last.then_inc(t_t, 1)

                def head_outputs(c, gi, par):
                    pe.wait_ge(a_t, 3 * c + 3)
                    o = B[4][:, :].rearrange("p (r q) -> p r q", r=2)
                    for e in range(2):
                        mm(o, vpad[par][0][:, 64 - 64 * e:192 - 64 * e],
                           pt0[:, e::2, :], start=(e == 0), stop=False, skip_group_check=True)
                    for e in range(2):
                        last = mm(o[:, :, P:SEQ], vpad[par][1][:, 64 - 64 * e:192 - 64 * e], pt1[:, e::2, :],
                                  start=False, stop=(e == 1), skip_group_check=True)
                    last.then_inc(t_o, 1)

                def out_projection(c, gi, b):
                    pe.wait_ge(v_o, c + 1)
                    if gi == 0 and not (isinstance(b, int) and b == 0):
                        pe.wait_ge(v_ux, b)
                    for j in range(2):
                        for r in range(2):
                            q = slice(j * P, (j + 1) * P)
                            last = split3(mm, B[5][:, j * HID:(j + 1) * HID], oth[gi % 2][:, r, q], otl[gi % 2][:, r, q],
                                          wvo_h[:, 2 * gi + r, :], wvo_l[:, 2 * gi + r, :],
                                          gi == 0 and j == 0 and r == 0, gi == NHG - 1 and r == 1,
                                          skip_group_check=True)
                    last.then_inc(t_p, 1)

                pe.wait_ge(v_x, NT)
                pe.wait_ge(sp_a1, 6 * 16)
                pe.wait_ge(v_pad, 1)
                transpose_x(0)
                query_weights(0)
                down_projections(0)
                query_weights(1)
                transpose_latents(0)
                pe.wait_ge(sp_a2, 3 * 16)
                output_weights()
                pe.wait_ge(v_aw, 6)
                for j in range(2):
                    pe.wait_ge(v_at, j + 1)
                    queries(0, 0, j)
                for j in range(2):
                    transpose_queries(0, j)
                pe.wait_ge(v_aw, 10)

                def sequence(b, par, first, last):
                    for gi in range(NHG):
                        c = NHG * b + gi
                        end = last and gi == NHG - 1
                        if gi and not last:
                            pe.wait_ge(v_qt, 2 * c + 2)
                            (transpose_x, down_projections, transpose_latents)[gi - 1](b + 1)
                        for u in range(NUNIT):
                            scores(c, u, par)
                        for j in range(2):
                            if end:
                                break
                            if gi == 0 or last:
                                pe.wait_ge(v_qt, 2 * c + j + 1)
                            else:
                                pe.wait_ge((v_ax, a_qa, v_at)[gi - 1], 2 * b + j + 3)
                            queries((gi + 1) % NHG, par if gi < NHG - 1 else 1 - par, j)
                        if not (first and gi == 0):
                            head_outputs(c - 1, (gi - 1) % NHG, par if gi else 1 - par)
                        if not end:
                            transpose_queries(c + 1, 0)
                        transpose_probs(c, 0)
                        if not end:
                            transpose_queries(c + 1, 1)
                        if not (first and gi == 0):
                            out_projection(c - 1, (gi - 1) % NHG, b if gi else b - 1)
                        transpose_probs(c, 1)
                        transpose_probs(c, 2)

                pairs(pe, 0, NSEQ - 1, sequence)
                c = NHG * NSEQ - 1
                head_outputs(c, NHG - 1, (NSEQ - 1) % 2)
                out_projection(c, NHG - 1, NSEQ - 1)

            ffn(0)
            attention()
            ffn(1)

        @block.scalar
        def _(act):
            copy, fn = nc.scalar.copy, nc.scalar.activation

            def ffn(f):
                t0 = NT * f

                def high_x(t, par):
                    act.wait_ge(t_xt, t + 1)
                    copy(xh[par][:, :, :], B[7][:, 0:HID].rearrange("p (k n) -> p k n", k=KH)).then_inc(a_xh, 1)

                def high_hidden(n, g):
                    act.wait_ge(t_ht, n + 1)
                    if not (isinstance(n, int) and n < 2):
                        act.wait_ge(t_dn, n - 1)
                    full = sum(w == P for _, w in CH[g])
                    bank = B[4 + g % 2][:, :].rearrange("p (c n) -> p c n", n=P)
                    last = copy(hth[:, g % 2, 0:full, :], bank[:, 0:full, :])
                    if full < len(CH[g]):
                        w = CH[g][full][1]
                        last = copy(hth[0:w, g % 2, full, :], bank[0:w, full, :])
                    last.then_inc(a_hh, 1)

                def high_weights(*keys):
                    for key in keys:
                        i, (kind, g) = uidx[key], key
                        act.wait_ge(sp_w[i], 32 if key == ("d", NG - 1) else 16)
                        src, dst = unit_raw(i), unit_dst(i, 0)
                        full = sum(w == P for _, w in CH[g]) if kind == "d" else KH
                        last = copy(dst[:, 0:full, :], src[:, 0:full, :])
                        if kind == "d" and full < len(CH[g]):
                            w = CH[g][full][1]
                            last = copy(dst[0:w, full, :], src[0:w, full, :])
                        last.then_inc(a_wh, 1)

                if f == 1:
                    act.wait_ge(v_ux, NSEQ)
                nc.scalar.preload_act_table(ACT.Silu)
                high_x(t0, 0)
                if f == 0:
                    high_weights(*units[0:4])

                def tile(i, par, first, last):
                    t = i + t0
                    for g in range(NG):
                        n = t * NG + g
                        act.wait_ge(t_g, n + 1)
                        if not (isinstance(n, int) and n < 2):
                            act.wait_ge(v_h, n - 1)
                        fn(silu[:, g % 2, 0:GWID[g]], B[g % 2][:, 0:GWID[g]], ACT.Silu).then_inc(a_sl, 1)
                        if g == 1 and not last:
                            high_x(t + 1, 1 - par)
                        if not (first and g == 0):
                            high_hidden(n - 1, (g - 1) % NG)
                        if f == 0 and first:
                            high_weights(*units[WCUT[g]:WCUT[g + 1]])
                    if f == 0 and first:
                        act.wait_ge(sp_qa, 16)
                        copy(wqa_h[:, :, :], wqa_raw[:, :, :]).then_inc(a_wh, 1)

                pairs(act, 0, NT - 1, tile)
                high_hidden((t0 + NT) * NG - 1, NG - 1)

            act.wait_ge(sp_gate, 16)
            copy(gate_h[:, :, :], gate_raw[:, :, :]).then_inc(a_wh, 1)
            ffn(0)

            def attention():
                def high_x(b):
                    for j in range(2):
                        act.wait_ge(t_ax, 2 * b + j + 1)
                        copy(xh[j][:, :, :], B[6 + j][:, 0:HID].rearrange("p (k n) -> p k n", k=KH)).then_inc(a_ax, 1)

                def copy_latents(b):
                    for j in range(2):
                        act.wait_ge(t_qa, 2 * b + j + 1)
                        copy(qa[:, j, :], B[6 + j][:, 0:QA]).then_inc(a_qa, 1)

                def mean_squares(b):
                    act.wait_ge(a_qa, 2 * b + 2)
                    for j in range(2):
                        for i, (a, w) in enumerate(((0, QLR), (QLR, KVL))):
                            last = fn(cq[:, j, :, :].rearrange("p k n -> p (k n)")[:, a:a + w], qa[:, j, a:a + w], ACT.Square, scale=float(w) ** -0.5,
                                      accum_out=ms[:, j, i:i + 1])
                    last.then_inc(a_ms, 1)

                def high_latents(b, par):
                    for j in range(2):
                        act.wait_ge(t_at, 2 * b + j + 1)
                        copy(th[par][:, :, j, :], B[6 + j][:, 0:3 * P].rearrange("p (k n) -> p k n", k=3)).then_inc(a_at, 1)

                def copy_queries(c):
                    for j in range(2):
                        act.wait_ge(t_q, 2 * c + j + 1)
                        copy(qsb[:, j, :, 0:KVL],
                             B[6 + j][:, :].rearrange("p (h n) -> p h n", h=HG)[:, :, 0:KVL]).then_inc(a_q, 1)

                def high_queries(c, j):
                    act.wait_ge(t_qt, 2 * c + j + 1)
                    copy(qth[:, j, :, :], B[6 + j][:, :].rearrange("p (h n) -> p h n", h=HG)).then_inc(a_qt, 1)

                def exponentials(c, u):
                    m = 3 * c + u
                    act.wait_ge(v_m, m + 1)
                    if not (isinstance(c, int) and c == 0):
                        act.wait_ge(t_t, m - 2)
                    nh = 4 if u == 0 else 2
                    w = 512 // nh
                    for i in range(nh):
                        last = fn(prob[:, u, i * w:(i + 1) * w], B[u][:, i * w:(i + 1) * w], ACT.Exp,
                                  bias=nmax[:, u, i:i + 1], accum_out=rsum[:, u, i:i + 1])
                    last.then_inc(a_e, 1)

                def copy_probs(c, u):
                    act.wait_ge(t_t, 3 * c + u + 1)
                    bank = B[PROB_BANK[u]][:, :].rearrange("p (h n) -> p h n", h=HG)
                    if u == 0:
                        last = copy(pt0[:, :, 0:P], bank)
                    else:
                        hs = slice(2 * u - 2, 2 * u)
                        copy(pt0[:, hs, P:SEQ], bank[:, 0:2, :])
                        last = copy(pt1[:, hs, :], bank[:, 2:4, :])
                    last.then_inc(a_t, 1)

                def high_outputs(c, gi):
                    act.wait_ge(t_o, c + 1)
                    copy(oth[gi % 2][:, :, :], B[4][:, :].rearrange("p (r q) -> p r q", r=2)).then_inc(a_o, 1)

                def high_query_weights(c):
                    w = (wq1_h, wq2)[c][:, :].rearrange("p (h n) -> p h n", h=NH)
                    for i in range(2):
                        act.wait_ge(t_w, 2 * c + i + 1)
                        fn(w[:, 8 * i:8 * i + 8, 0:KVL], B[2 * c + i][:, :].rearrange("p (h n) -> p h n", h=8), ACT.Copy,
                           scale=qs2[:, c:c + 1]).then_inc(a_w, 1)

                act.wait_ge(v_x, NT)
                nc.scalar.preload_act_table(ACT.Exp)
                act.wait_ge(v_pad, 1)
                for c, raw in enumerate((rot1_raw, rot2_raw)):
                    w = (wq1_h, wq2)[c][:, :].rearrange("p (h n) -> p h n", h=NH)
                    fn(w[:, :, KVL:P], raw[:, :, :], ACT.Copy, scale=qs2[:, c:c + 1]).then_inc(a_w, 1)
                high_x(0)
                high_query_weights(0)
                copy_latents(0)
                mean_squares(0)
                high_query_weights(1)
                high_latents(0, 0)
                for q, bank in enumerate((4, 5, 0, 1)):
                    act.wait_ge(t_w, 5 + q)
                    fn(wvo_h[:, 2 * q:2 * q + 2, :], B[bank][:, :].rearrange("p (r n) -> p r n", r=2), ACT.Copy,
                       scale=kvln2[:, 0:1]).then_inc(a_w, 1)
                copy_queries(0)
                high_queries(0, 0)
                high_queries(0, 1)

                def sequence(b, par, first, last):
                    for gi in range(NHG):
                        c = NHG * b + gi
                        end = last and gi == NHG - 1
                        if not last:
                            if gi == 1:
                                high_x(b + 1)
                            if gi == 2:
                                copy_latents(b + 1)
                            if gi == 3:
                                high_latents(b + 1, 1 - par)
                        exponentials(c, 0)
                        exponentials(c, 1)
                        if not end:
                            copy_queries(c + 1)
                        exponentials(c, 2)
                        if gi == 2 and not last:
                            mean_squares(b + 1)
                        if not (first and gi == 0):
                            high_outputs(c - 1, (gi - 1) % NHG)
                        if not end:
                            high_queries(c + 1, 0)
                        copy_probs(c, 0)
                        if not end:
                            high_queries(c + 1, 1)
                        copy_probs(c, 1)
                        copy_probs(c, 2)

                pairs(act, 0, NSEQ - 1, sequence)
                high_outputs(NHG * NSEQ - 1, NHG - 1)

            attention()
            ffn(1)

        @block.vector
        def _(dve):
            V = nc.vector
            link = Link(dve, v_link)
            linked = [0]

            def minus(out_, a, hi):
                return V.tensor_tensor(out_, a, hi.bitcast(F32), ALU.subtract)

            def ffn(f):
                t0 = NT * f

                def variance(t):
                    V.bn_stats(st6[:, :], x[:, t - t0, :]).then_inc(v_link, 1)
                    link.n += 1
                    dve.wait_ge(v_link, link.base + link.n)
                    dve.sem_inc(v_turn, 1)
                    link(V.bn_aggr(mv[:, :], st6[:, :]))
                    V.tensor_scalar(ve[:, :], mv[:, 1:2], LN_EPS, None, ALU.add).then_inc(v_st, 1)

                def normalise(t):
                    dve.wait_ge(g_rs, t + 1)
                    V.tensor_scalar(xn[:, 0, :], x[:, t - t0, :], mv[:, 0:1], rstd[:, 0:1], ALU.subtract,
                                    ALU.mult).then_inc(v_xn, 1)

                def low_x(t, par):
                    dve.wait_ge(a_xh, t + 1)
                    minus(xl[par][:, :, :], B[7][:, 0:HID].rearrange("p (k n) -> p k n", k=KH),
                          xh[par][:, :, :]).then_inc(v_xl, 1)

                def negate_logits(t):
                    dve.wait_ge(t_lg, t + 1)
                    V.tensor_scalar(nl[:, :], B[7][:, 256:256 + NE], -1.0, None, ALU.mult).then_inc(v_nl, 1)

                def expert_weights(t, par):
                    dve.wait_ge(g_en, t + 1)
                    link(V.tensor_scalar(en1[:, :], en[:, :], 1.0, None, ALU.add))
                    link(V.reciprocal(sg[:, :], en1[:, :]))
                    other = sg[:, :].unsqueeze(1).broadcast_to([P, NE, NE])
                    own = sg[:, :].unsqueeze(2).broadcast_to([P, NE, NE])
                    V.tensor_tensor(cgt[:, :, :], other, own, ALU.is_gt)
                    link(V.tensor_tensor(cge[:, :, :], other, own, ALU.is_ge))
                    link(V.tensor_tensor(cgl[:, :, :], cge[:, :, :], tri8[:, :, :], ALU.mult))
                    link(V.tensor_tensor(cbt[:, :, :], cgl[:, :, :], cgt[:, :, :], ALU.max))
                    link(V.tensor_reduce(cnt[:, :], cbt[:, :, :], AX.X, ALU.add))
                    link(V.scalar_tensor_tensor(msk[:, :], cnt[:, :], 2.0, sg[:, :], ALU.is_lt, ALU.mult,
                                                accum_out=den[:, 0:1]))
                    link(V.tensor_scalar(den[:, 1:2], den[:, 0:1], 1e-20, None, ALU.add))
                    link(V.reciprocal(den[:, 2:3], den[:, 1:2]))
                    V.tensor_scalar(wgt[:, par, :], msk[:, :], den[:, 2:3], TOPK_SCALE, ALU.mult,
                                    ALU.mult).then_inc(v_wt, 1)

                def middle(n, g, par, t):
                    dve.wait_ge(t_u, n + 1)
                    dve.wait_ge(a_sl, n + 1)
                    if g == 0:
                        dve.wait_ge(v_wt, t + 1)
                    if not (isinstance(n, int) and n < 2):
                        dve.wait_ge(t_ht, n - 1)
                    for a, w, e in segments(g):
                        s_, u_ = silu[:, g % 2, a:a + w], B[2 + g % 2][:, a:a + w]
                        if e is None:
                            last = V.tensor_tensor(hid[:, g % 2, a:a + w], s_, u_, ALU.mult)
                        else:
                            last = V.scalar_tensor_tensor(hid[:, g % 2, a:a + w], s_, wgt[:, par, e:e + 1], u_,
                                                          ALU.mult, ALU.mult)
                    last.then_inc(v_h, 1)

                def low_hidden(n, g):
                    dve.wait_ge(a_hh, n + 1)
                    full = sum(w == P for _, w in CH[g])
                    bank = B[4 + g % 2][:, :].rearrange("p (c n) -> p c n", n=P)
                    last = minus(htl[:, g % 2, 0:full, :], bank[:, 0:full, :], hth[:, g % 2, 0:full, :])
                    if full < len(CH[g]):
                        w = CH[g][full][1]
                        last = minus(htl[0:w, g % 2, full, :], bank[0:w, full, :], hth[0:w, g % 2, full, :])
                    last.then_inc(v_hl, 1)

                def add_to_x(t):
                    dve.wait_ge(t_dn, (t + 1) * NG)
                    V.scalar_tensor_tensor(x[:, t - t0, :], B[6][:, 0:HID], 0.5, x[:, t - t0, :], ALU.mult,
                                           ALU.add).then_inc(v_x, 1)

                def low_weights(*keys):
                    for kind, g in keys:
                        i = uidx[(kind, g)]
                        if lo_on_pool(i):
                            continue
                        dve.wait_ge(a_wh, i + 2)
                        src, hi, lo = unit_raw(i), unit_dst(i, 0), unit_dst(i, 1)
                        full = sum(w == P for _, w in CH[g]) if kind == "d" else KH
                        last = minus(lo[:, 0:full, :], src[:, 0:full, :], hi[:, 0:full, :])
                        if kind == "d" and full < len(CH[g]):
                            w = CH[g][full][1]
                            last = minus(lo[0:w, full, :], src[0:w, full, :], hi[0:w, full, :])
                        last.then_inc(v_wl, 1)

                link.at(linked[0])
                variance(t0)
                normalise(t0)
                low_x(t0, 0)
                if f == 0:
                    low_weights(*units[0:4])
                negate_logits(t0)
                expert_weights(t0, 0)
                start = linked[0] + link.n
                per = link.n

                def tile(i, par, first, last):
                    t = i + t0
                    link.at(i * per + start)
                    for g in range(NG):
                        n = t * NG + g
                        if g == 0 and not last:
                            variance(t + 1)
                        middle(n, g, par, t)
                        if f == 0 and first:
                            low_weights(*units[WCUT[g]:WCUT[g + 1]])
                        if not (first and g == 0):
                            if g == 1 and not last:
                                low_x(t + 1, 1 - par)
                            low_hidden(n - 1, (g - 1) % NG)
                        if g == 0 and not last:
                            normalise(t + 1)
                        if g == 1 and not first:
                            add_to_x(t - 1)
                        if g == 2 and not last:
                            negate_logits(t + 1)
                        if g == 3 and not last:
                            expert_weights(t + 1, 1 - par)
                    assert last or link.n == per
                    if f == 0 and first:
                        dve.wait_ge(a_wh, len(units) + 2)
                        minus(wqa_l[:, :, :], wqa_raw[:, :, :], wqa_h[:, :, :]).then_inc(v_wl, 1)
                        dve.wait_ge(sp_x, 32)
                        dve.wait_ge(sp_c2, 6 * 16)
                    if f == 0 and last:
                        dve.wait_ge(sp_a1, 6 * 16)
                        V.tensor_scalar(qs2[:, :], qs[:, :], SM_SCALE, None, ALU.mult)
                        V.tensor_tensor(kvbk_raw[:, :, :], kvbk_raw[:, :, :],
                                        kvln_row[:, :].unsqueeze(1).broadcast_to([P, NH, KVL]), ALU.mult)
                        V.memset(kvbv_raw[:, :, 64:128], 0.0).then_inc(v_pad, 1)

                pairs(dve, 0, NT - 1, tile)
                low_hidden((t0 + NT) * NG - 1, NG - 1)
                add_to_x(t0 + NT - 1)
                linked[0] = start + (NT - 1) * per

            V.memset(mhalf[:, :], -0.5)
            V.memset(ebase[:, :], float(np.e)).then_inc(v_one, 1)
            dve.wait_ge(a_wh, 1)
            minus(gate_l[:, :, :], gate_raw[:, :, :], gate_h[:, :, :]).then_inc(v_wl, 1)
            dve.wait_ge(sp_x0, 16)
            dve.wait_ge(sp_c, 2 * 16)
            ffn(0)

            def attention():
                def variances(b):
                    for j in range(2):
                        V.bn_stats(ast6[:, j, :], x[:, TPS * b + j, :]).then_inc(v_link, 1)
                    link.n += 2
                    dve.wait_ge(v_link, link.base + link.n)
                    dve.sem_inc(v_turn, 1)
                    for j in range(2):
                        V.bn_aggr(amv[:, j, :], ast6[:, j, :]).then_inc(v_link, 1)
                    link.n += 2
                    dve.wait_ge(v_link, link.base + link.n)
                    V.tensor_scalar(ave[:, :], amv[:, :, 1], LN_EPS, None, ALU.add).then_inc(v_ast, 1)

                def normalise(b):
                    dve.wait_ge(g_ars, b + 1)
                    for j in range(2):
                        last = V.tensor_scalar(xn[:, j, :], x[:, TPS * b + j, :], amv[:, j, 0:1], arstd[:, j:j + 1],
                                               ALU.subtract, ALU.mult)
                    last.then_inc(v_axn, 1)

                def low_x(b):
                    for j in range(2):
                        dve.wait_ge(a_ax, 2 * b + j + 1)
                        minus(xl[j][:, :, :], B[6 + j][:, 0:HID].rearrange("p (k n) -> p k n", k=KH),
                              xh[j][:, :, :]).then_inc(v_ax, 1)

                def squares_eps(b):
                    dve.wait_ge(a_ms, b + 1)
                    V.tensor_scalar(mse[:, :, :], ms[:, :, :], RMS_EPS, None, ALU.add).then_inc(v_ms, 1)

                def latents(b, par):
                    dve.wait_ge(g_rr, b + 1)
                    half = DR // 2
                    kpe = qa[:, :, QLR + KVL:QA]
                    V.tensor_tensor(kr[:, :, 0, :], kpe, cos[:, :, :], ALU.mult)
                    V.tensor_tensor(kr[:, :, 1, 0:half], kpe[:, :, half:DR], sin[:, :, 0:half], ALU.mult)
                    link(V.tensor_tensor(kr[:, :, 1, half:DR], kpe[:, :, 0:half], sin[:, :, half:DR], ALU.mult))
                    for j in range(2):
                        r0, r1 = rr[:, j, 0:1], rr[:, j, 1:2]
                        flat = cq[:, j, :, :].rearrange("p k n -> p (k n)")
                        V.tensor_scalar(flat[:, 0:QLR], qa[:, j, 0:QLR], r0, None, ALU.mult)
                        V.tensor_scalar(flat[:, QLR:2 * P], qa[:, j, P:QLR], r0, None, ALU.mult)
                        V.tensor_scalar(flat[:, 2 * P:2 * P + KVL], qa[:, j, QLR:QLR + KVL], r1, None, ALU.mult)
                        V.tensor_scalar(vpad[par][j][:, KVL:2 * KVL], qa[:, j, QLR:QLR + KVL], r1, None, ALU.mult)
                    V.tensor_tensor(cq[:, :, 2, KVL:P], kr[:, :, 0, :], kr[:, :, 1, :], ALU.add).then_inc(v_cq, 1)

                def low_latents(b, par):
                    for j in range(2):
                        dve.wait_ge(a_at, 2 * b + j + 1)
                        minus(tl[par][:, :, j, :], B[6 + j][:, 0:3 * P].rearrange("p (k n) -> p k n", k=3),
                              th[par][:, :, j, :]).then_inc(v_at, 1)

                def rotate_queries(c):
                    half = DR // 2
                    for j in range(2):
                        dve.wait_ge(t_q, 2 * c + j + 1)
                        dve.wait_ge(a_q, 2 * c + j + 1)
                        pe_part = B[6 + j][:, :].rearrange("p (h n) -> p h n", h=HG)[:, :, KVL:P]

                        def table(tab, a, w):
                            return tab[:, j, a:a + w].unsqueeze(1).broadcast_to([P, HG, w])

                        V.tensor_tensor(qsb[:, j, :, KVL:P], pe_part, table(cos, 0, DR), ALU.mult)
                        V.tensor_tensor(rt2[:, j, :, 0:half], pe_part[:, :, half:DR], table(sin, 0, half), ALU.mult)
                        V.tensor_tensor(rt2[:, j, :, half:DR], pe_part[:, :, 0:half], table(sin, half, half),
                                        ALU.mult).then_inc(v_q, 1)

                def low_queries(c):
                    for j in range(2):
                        dve.wait_ge(a_qt, 2 * c + j + 1)
                        minus(qtl[:, j, :, :], B[6 + j][:, :].rearrange("p (h n) -> p h n", h=HG),
                              qth[:, j, :, :]).then_inc(v_qt, 1)

                def maxima(c, u):
                    dve.wait_ge(t_s, 3 * c + u + 1)
                    nh = 4 if u == 0 else 2
                    s_ = B[u][:, :].rearrange("p (h n) -> p h n", h=nh)
                    diag = s_ if u == 0 else s_[:, :, P:SEQ]
                    link(V.tensor_tensor(diag, diag, mask[:, :].unsqueeze(1).broadcast_to([P, nh, P]), ALU.add))
                    V.tensor_reduce(nmax[:, u, 0:nh], s_, AX.X, ALU.max, negate=True).then_inc(v_m, 1)

                def reciprocals(c, u):
                    dve.wait_ge(a_e, 3 * c + u + 1)
                    nh = 4 if u == 0 else 2
                    V.reciprocal(rcp[:, u, 0:nh], rsum[:, u, 0:nh]).then_inc(v_r, 1)

                def low_outputs(c, gi):
                    dve.wait_ge(a_o, c + 1)
                    minus(otl[gi % 2][:, :, :], B[4][:, :].rearrange("p (r q) -> p r q", r=2),
                          oth[gi % 2][:, :, :]).then_inc(v_o, 1)

                def add_to_x(b):
                    dve.wait_ge(t_p, NHG * b + NHG)
                    V.tensor_tensor(x[:, bass.ds(TPS * b, TPS), :], B[5][:, :].rearrange("p (j n) -> p j n", j=TPS),
                                    x[:, bass.ds(TPS * b, TPS), :], ALU.add).then_inc(v_ux, 1)

                def low_part(w_l, w_h, src, scale, n):
                    dve.wait_ge(a_w, n)
                    V.scalar_tensor_tensor(w_l, src, scale, w_h.bitcast(F32), ALU.mult, ALU.subtract).then_inc(v_aw, 1)

                def low_query_weights(c, part):
                    r = slice(0, P) if c == 0 else slice(64, P)
                    hi = (wq1_h, wq2)[c][:, :].rearrange("p (h n) -> p h n", h=NH)[r]
                    lo = (wq1_l, wq2)[c][:, :].rearrange("p (h n) -> p h n", h=NH)[r]
                    if part == 2:
                        cs, hs, src, n = slice(KVL, P), slice(0, NH), (rot1_raw, rot2_raw)[c][r], c + 1
                    else:
                        cs, hs, n = slice(0, KVL), slice(8 * part, 8 * part + 8), 2 * c + part + 3
                        src = B[2 * c + part][r, :].rearrange("p (h n) -> p h n", h=8)
                    low_part(lo[:, hs, cs], hi[:, hs, cs], src, qs2[r, c:c + 1], n)

                link.at(linked[0])
                for i in range(2):
                    for j in range(2):
                        V.memset(vpad[i][j][:, 0:KVL], 0.0)
                        V.memset(vpad[i][j][:, 2 * KVL:3 * KVL], 0.0)
                variances(0)
                normalise(0)
                low_x(0)
                low_query_weights(0, 0)
                low_query_weights(0, 1)
                squares_eps(0)
                low_query_weights(0, 2)
                latents(0, 0)
                low_query_weights(1, 0)
                low_query_weights(1, 1)
                low_query_weights(1, 2)
                low_latents(0, 0)
                for q, bank in enumerate((4, 5, 0, 1)):
                    low_part(wvo_l[:, 2 * q:2 * q + 2, :], wvo_h[:, 2 * q:2 * q + 2, :],
                             B[bank][:, :].rearrange("p (r n) -> p r n", r=2), kvln2[:, 0:1], 7 + q)
                rotate_queries(0)
                low_queries(0)
                start = linked[0] + link.n
                per = 5 + 3 * NHG

                def sequence(b, par, first, last):
                    link.at(b * per + start)
                    for gi in range(NHG):
                        c = NHG * b + gi
                        end = last and gi == NHG - 1
                        if not last:
                            if gi == 0:
                                variances(b + 1)
                            if gi == 1:
                                low_x(b + 1)
                            if gi == 3:
                                low_latents(b + 1, 1 - par)
                        for u in range(NUNIT):
                            maxima(c, u)
                        reciprocals(c, 0)
                        if not end:
                            rotate_queries(c + 1)
                        reciprocals(c, 1)
                        reciprocals(c, 2)
                        if gi == 2 and not last:
                            squares_eps(b + 1)
                        if not (first and gi == 0):
                            low_outputs(c - 1, (gi - 1) % NHG)
                        if not end:
                            low_queries(c + 1)
                        if gi == 0 and not last:
                            normalise(b + 1)
                        if gi == 2 and not last:
                            latents(b + 1, 1 - par)
                        if gi == 0 and not first:
                            add_to_x(b - 1)
                    assert last or link.n == per, link.n

                pairs(dve, 0, NSEQ - 1, sequence)
                low_outputs(NHG * NSEQ - 1, NHG - 1)
                add_to_x(NSEQ - 1)
                linked[0] = start + (NSEQ - 1) * per + link.n

            attention()
            dve.wait_ge(v_ux, NSEQ)
            ffn(1)

        @block.gpsimd
        def _(pool):
            G = nc.gpsimd

            def ffn(f):
                t0 = NT * f

                def rstd_of(t):
                    pool.wait_ge(v_st, t + 1)
                    G.tensor_tensor(rstd[:, :], ve[:, :], mhalf[:, 0:1], ALU.pow).then_inc(g_rs, 1)

                def exp_of(t):
                    pool.wait_ge(v_nl, t + 1)
                    G.tensor_tensor(en[:, :], ebase[:, :], nl[:, :], ALU.pow).then_inc(g_en, 1)

                def low_weights(*keys):
                    for key in keys:
                        i = uidx[key]
                        if lo_on_pool(i):
                            pool.wait_ge(a_wh, i + 2)
                            G.tensor_tensor(unit_dst(i, 1), unit_raw(i), unit_dst(i, 0).bitcast(F32),
                                            ALU.subtract).then_inc(g_wl, 1)

                rstd_of(t0)
                if f == 0:
                    low_weights(*units[0:2])
                exp_of(t0)

                def tile(i, par, first, last):
                    if f == 0 and first:
                        low_weights(*units[2:WCUT[0]])
                    if not last:
                        rstd_of(i + t0 + 1)
                    if f == 0 and first:
                        low_weights(*units[WCUT[0]:WCUT[2]])
                    if not last:
                        exp_of(i + t0 + 1)
                    if f == 0 and first:
                        low_weights(*units[WCUT[2]:])

                pairs(pool, 0, NT - 1, tile)

            pool.wait_ge(v_one, 1)
            ffn(0)

            def attention():
                def rstd_of(b):
                    pool.wait_ge(v_ast, b + 1)
                    G.tensor_tensor(arstd[:, :], ave[:, :], mhalf[:, 0:2], ALU.pow).then_inc(g_ars, 1)

                def rms_of(b):
                    pool.wait_ge(v_ms, b + 1)
                    G.tensor_tensor(rr[:, :, :].rearrange("p j i -> p (j i)"), mse[:, :, :].rearrange("p j i -> p (j i)"),
                                    mhalf[:, 0:4], ALU.pow).then_inc(g_rr, 1)

                def add_rotation(c):
                    for j in range(2):
                        pool.wait_ge(v_q, 2 * c + j + 1)
                        G.tensor_tensor(qsb[:, j, :, KVL:P], qsb[:, j, :, KVL:P], rt2[:, j, :, :], ALU.add).then_inc(g_q, 1)

                def probabilities(c, u):
                    pool.wait_ge(v_r, 3 * c + u + 1)
                    nh = 4 if u == 0 else 2
                    place = prob[:, u, :].rearrange("p (h n) -> p h n", h=nh)
                    G.tensor_tensor(place, place, rcp[:, u, 0:nh].unsqueeze(2).broadcast_to([P, nh, 512 // nh]),
                                    ALU.mult).then_inc(g_n, 1)

                rstd_of(0)
                rms_of(0)
                add_rotation(0)

                def sequence(b, par, first, last):
                    for gi in range(NHG):
                        c = NHG * b + gi
                        if gi == 0 and not last:
                            rstd_of(b + 1)
                        probabilities(c, 0)
                        if not (last and gi == NHG - 1):
                            add_rotation(c + 1)
                        probabilities(c, 1)
                        if gi == 2 and not last:
                            rms_of(b + 1)
                        probabilities(c, 2)

                pairs(pool, 0, NSEQ - 1, sequence)

            attention()
            ffn(1)


def kernel(**inputs):
    import concourse.bacc as bacc
    from concourse.bass_utils import run_bass_kernel_spmd

    a = {k.replace("L0_", ""): np.asarray(v) for k, v in inputs.items()}
    qb = a["attn_w_qb"].reshape(NH, DN + DR, QLR)
    kvb = a["attn_w_kvb"].reshape(NH, DN + DV, KVL)
    qln, kvln = a["attn_q_a_ln_w"], a["attn_kv_a_ln_w"]
    inv = (np.float32(1.0) / np.float32(10000.0) ** (np.arange(0, DR, 2, dtype=np.float32) / np.float32(DR))).astype(np.float32)
    ang = np.outer(np.arange(SEQ, dtype=np.float32), inv).astype(np.float32)
    cos, sin = np.cos(ang), np.sin(ang)

    def tiles(t):
        return t.reshape(TPS, P, DR).transpose(1, 0, 2)

    arrays = {
        "x": a["attn_hidden_states"],
        "gate": a["ffn_gate_w"].T,
        "wg": np.concatenate([a["ffn_exp_wg"].reshape(NE * EFF, HID), a["ffn_shared_wg"]]).T,
        "wu": np.concatenate([a["ffn_exp_wu"].reshape(NE * EFF, HID), a["ffn_shared_wu"]]).T,
        "wd": np.concatenate([a["ffn_exp_wd"].transpose(0, 2, 1).reshape(NE * EFF, HID), a["ffn_shared_wd"].T]),
        "wqa": np.concatenate([a["attn_w_qa"], a["attn_w_kva"]]).T,
        "wqbn": qb[:, :DN].transpose(1, 0, 2),
        "wqbp": qb[:, DN:].transpose(2, 0, 1),
        "kvbk": kvb[:, :DN].transpose(1, 0, 2),
        "kvbv": kvb[:, DN:].transpose(1, 0, 2),
        "wo": a["attn_w_o"].reshape(HID, NH, DV).transpose(2, 1, 0),
        "qln": np.stack([qln[0:P], np.concatenate([qln[P:QLR], qln[P:QLR]])], axis=1),
        "kvln2": np.concatenate([kvln, kvln])[:, None],
        "kvln_row": np.repeat(kvln[None, :], P, axis=0),
        "ident": np.eye(P, dtype=np.float32),
        "mask": np.where(np.arange(P)[None, :] <= np.arange(P)[:, None], 0.0, -1e30).astype(np.float32),
        "tri8": np.repeat(np.tri(NE, NE, -1, dtype=np.float32)[None], P, axis=0),
        "cos": tiles(np.concatenate([cos, cos], axis=1)),
        "sin": tiles(np.concatenate([-sin, sin], axis=1)),
    }
    arrays = {k: np.ascontiguousarray(v) for k, v in arrays.items()}
    nc = bacc.Bacc("TRN2", target_bir_lowering=False, num_devices=1, dynamic_dma_scratch_size=2048)
    d = {k: nc.dram_tensor("in_" + k, v.shape, F32, kind="ExternalInput").ap() for k, v in arrays.items()}
    out = nc.dram_tensor("out", arrays["x"].shape, F32, kind="ExternalOutput").ap()
    build(nc, d, out)
    r = run_bass_kernel_spmd(nc, [{"in_" + k: v for k, v in arrays.items()}], core_ids=[0])
    return r.results[0]["out"]
```

```python
from contextlib import ExitStack

import numpy as np

import concourse.bass as bass
from concourse import mybir

F32 = mybir.dt.float32
F32R = mybir.dt.float32r
ALU = mybir.AluOpType
ACT = mybir.ActivationFunctionType
AX = mybir.AxisListType

P = 128
HID = 256
KH = HID // P
NSEQ, SEQ = 8, 256
TPS = SEQ // P
NT = NSEQ * TPS
NE, EFF, SFF = 8, 176, 352
FF = NE * EFF + SFF
GW = 512
NG = 1 + -(-NE * EFF // GW)
GOFF = [0] + list(range(SFF, FF, GW))
GWID = [b - a for a, b in zip(GOFF, GOFF[1:] + [FF])]
CH = [[(c, min(P, GWID[g] - c)) for c in range(0, GWID[g], P)] for g in range(NG)]
CB = [sum(len(c) for c in CH[:g]) for g in range(NG)]
NCH = sum(len(c) for c in CH)
TOPK_SCALE = 2.5
NH, QLR, KVL, DN, DR, DV = 16, 192, 64, 128, 64, 128
HG = 4
NHG = NH // HG
NUNIT = 3
SM_SCALE = float(DN + DR) ** -0.5
LN_EPS, RMS_EPS = 1e-5, 1e-6
QA = QLR + KVL + DR


class Link:

    def __init__(self, eng, sem):
        self.eng, self.sem, self.base, self.n = eng, sem, 0, 0

    def at(self, base):
        self.base, self.n = base, 0

    def __call__(self, ins):
        self.n += 1
        ins.then_inc(self.sem, 1)
        self.eng.wait_ge(self.sem, self.base + self.n)


def build(nc, d, out):
    with ExitStack() as ctx:
        def sb(name, shape, dt=F32, c=ctx):
            return c.enter_context(nc.sbuf_tensor(name, shape, dt))

        def sem(name):
            return ctx.enter_context(nc.semaphore(name))

        x = sb("x", [P, NT, HID])
        wg_h = sb("wg_h", [P, KH, NE + FF], F32R)
        wg_l = sb("wg_l", [P, KH, NE + FF], F32R)
        wu_h = sb("wu_h", [P, KH, FF], F32R)
        wu_l = sb("wu_l", [P, KH, FF], F32R)
        wd_h = sb("wd_h", [P, NCH, HID], F32R)
        wd_l = sb("wd_l", [P, NCH, HID], F32R)
        wq1_h = sb("wq1_h", [P, NH * P], F32R)
        wq1_l = sb("wq1_l", [P, NH * P], F32R)
        wq2 = sb("wq2", [P, NH * P], F32R)
        wvo_h = sb("wvo_h", [P, NH // 2, HID], F32R)
        wvo_l = sb("wvo_l", [P, NH // 2, HID], F32R)
        wqa_h = sb("wqa_h", [P, KH, QA], F32R)
        wqa_l = sb("wqa_l", [P, KH, QA], F32R)
        ident = sb("ident", [P, P])
        mask = sb("mask", [P, P])
        tri8 = sb("tri8", [P, NE, NE])
        cos = sb("cos", [P, TPS, DR])
        sin = sb("sin", [P, TPS, DR])
        kvln_row = sb("kvln_row", [P, KVL])
        kvln2 = sb("kvln2", [P, 1])
        qs = sb("qs", [P, 2])
        mhalf = sb("mhalf", [P, 4])
        ebase = sb("ebase", [P, NE])
        qs2 = sb("qs2", [P, 2])
        st6 = sb("st6", [P, 6])
        mv = sb("mv", [P, 2])
        ve = sb("ve", [P, 1])
        rstd = sb("rstd", [P, 1])
        xn = sb("xn", [P, 2, HID])

        xh = [sb(f"xh{i}", [P, KH, P], F32R) for i in range(2)]
        xl = [sb(f"xl{i}", [P, KH, P], F32R) for i in range(2)]
        low = ExitStack()
        silu = sb("silu", [P, 2, GW], c=low)
        hid = sb("hid", [P, 2, GW], c=low)
        hth = sb("hth", [P, 2, 4, P], F32R, c=low)
        htl = sb("htl", [P, 2, 4, P], F32R, c=low)
        nl = sb("nl", [P, NE], c=low)
        en = sb("en", [P, NE], c=low)
        en1 = sb("en1", [P, NE], c=low)
        sg = sb("sg", [P, NE], c=low)
        cgt = sb("cgt", [P, NE, NE], c=low)
        cge = sb("cge", [P, NE, NE], c=low)
        cgl = sb("cgl", [P, NE, NE], c=low)
        cbt = sb("cbt", [P, NE, NE], c=low)
        cnt = sb("cnt", [P, NE], c=low)
        msk = sb("msk", [P, NE], c=low)
        den = sb("den", [P, 3], c=low)
        wgt = sb("wgt", [P, 2, NE], c=low)
        stage = ExitStack()
        NRING = 8
        ring = sb("ring", [P, NRING, 1024], c=stage)
        wqa_raw = sb("wqa_raw", [P, KH, QA], c=stage)
        stage.close()
        stage = ExitStack()
        wqb_raw = sb("wqb_raw", [P, NH, 2 * P], c=stage)
        rot1_raw = sb("rot1_raw", [P, NH, DR], c=stage)
        rot2_raw = sb("rot2_raw", [P, NH, DR], c=stage)
        kvbk_raw = sb("kvbk_raw", [P, NH, KVL], c=stage)
        kvbv_raw = sb("kvbv_raw", [P, NH // 2, 192], c=stage)
        wo_raw = sb("wo_raw", [P, NH, HID], c=stage)
        stage.close()
        low.close()

        qa = sb("qa", [P, 2, QA])
        cq = sb("cq", [P, 2, 3, P])
        kr = sb("kr", [P, 2, 2, DR])
        ast6 = sb("ast6", [P, 2, 6])
        amv = sb("amv", [P, 2, 2])
        ave = sb("ave", [P, 2])
        arstd = sb("arstd", [P, 2])
        ms = sb("ms", [P, 2, 2])
        mse = sb("mse", [P, 2, 2])
        rr = sb("rr", [P, 2, 2])
        nmax = sb("nmax", [P, NUNIT, HG])
        rsum = sb("rsum", [P, NUNIT, HG])
        rcp = sb("rcp", [P, NUNIT, HG])
        vpad = [[sb(f"vpad{i}{j}", [P, 192]) for j in range(2)] for i in range(2)]
        qsb = sb("qsb", [P, 2, HG, P])
        th = [sb(f"th{i}", [P, 3, 2, P], F32R) for i in range(2)]
        tl = [sb(f"tl{i}", [P, 3, 2, P], F32R) for i in range(2)]
        rt2 = sb("rt2", [P, 2, HG, DR])
        qt0 = sb("qt0", [P, HG, P])
        kt0 = [sb(f"kt0{i}", [P, P]) for i in range(2)]
        qth = sb("qth", [P, HG, P], F32R)
        qtl = sb("qtl", [P, HG, P], F32R)
        prob = sb("prob", [P, NUNIT, 512])
        pt0 = sb("pt0", [P, HG, SEQ])
        pt1 = sb("pt1", [P, HG, P])
        oth = [sb(f"oth{i}", [P, 2, SEQ], F32R) for i in range(2)]
        otl = [sb(f"otl{i}", [P, 2, SEQ], F32R) for i in range(2)]

        B = [ctx.enter_context(nc.psum_tensor(f"B{i}", [P, 512], F32)) for i in range(8)]

        sp_x0 = sem("sp_x0")
        sp_x = sem("sp_x")
        sp_c = sem("sp_c")
        sp_c2 = sem("sp_c2")
        sp_w = [sem(f"sp_w{i}") for i in range(12)]
        sp_qa = sem("sp_qa")
        sp_a1 = sem("sp_a1")
        sp_a2 = sem("sp_a2")
        sp_out = sem("sp_out")
        a_wh = sem("a_wh")
        v_wl = sem("v_wl")
        g_wl = sem("g_wl")
        v_one = sem("v_one")
        v_link = sem("v_link")
        v_turn = sem("v_turn")
        v_st = sem("v_st")
        g_rs = sem("g_rs")
        v_xn = sem("v_xn")
        t_xt = sem("t_xt")
        a_xh = sem("a_xh")
        v_xl = sem("v_xl")
        a_nl = sem("a_nl")
        g_en = sem("g_en")
        v_wt = sem("v_wt")
        t_g = sem("t_g")
        t_u = sem("t_u")
        a_sl = sem("a_sl")
        v_h = sem("v_h")
        t_ht = sem("t_ht")
        a_hh = sem("a_hh")
        v_hl = sem("v_hl")
        t_dn = sem("t_dn")
        v_x = sem("v_x")
        v_pad = sem("v_pad")
        t_w = sem("t_w")
        a_w = sem("a_w")
        v_aw = sem("v_aw")
        v_ast = sem("v_ast")
        g_ars = sem("g_ars")
        v_axn = sem("v_axn")
        t_ax = sem("t_ax")
        a_ax = sem("a_ax")
        v_ax = sem("v_ax")
        t_qa = sem("t_qa")
        a_qa = sem("a_qa")
        a_ms = sem("a_ms")
        v_ms = sem("v_ms")
        g_rr = sem("g_rr")
        v_cq = sem("v_cq")
        t_at = sem("t_at")
        a_at = sem("a_at")
        v_at = sem("v_at")
        t_q = sem("t_q")
        a_q = sem("a_q")
        v_q = sem("v_q")
        g_q = sem("g_q")
        t_qt = sem("t_qt")
        a_qt = sem("a_qt")
        v_qt = sem("v_qt")
        t_s = sem("t_s")
        v_m = sem("v_m")
        a_e = sem("a_e")
        v_r = sem("v_r")
        g_n = sem("g_n")
        t_t = sem("t_t")
        a_t = sem("a_t")
        t_o = sem("t_o")
        a_o = sem("a_o")
        v_o = sem("v_o")
        t_p = sem("t_p")
        v_ux = sem("v_ux")

        units = []
        for g in range(NG):
            units += [("g", g), ("u", g)]
            if g >= 1:
                units.append(("d", g - 1))
        units.append(("d", NG - 1))
        uidx = {u: i for i, u in enumerate(units)}
        WCUT = [4, 7, 9, 11, 12]

        def unit_raw(i):
            kind, g = units[i]
            r = ring[:, i % NRING, :]
            if kind == "d":
                n = len(CH[g])
                return r[:, 0:n * HID].rearrange("p (c n) -> p c n", c=n)
            n = GWID[g] + extra(kind, g)
            return r[:, 0:KH * n].rearrange("p (k n) -> p k n", k=KH)

        def extra(kind, g):
            return NE if kind == "g" and g == 0 else 0

        def columns(kind, g):
            a = GOFF[g] + (NE if kind == "g" else 0)
            return slice(a - extra(kind, g), a + GWID[g])

        def unit_dst(i, lo):
            kind, g = units[i]
            if kind == "d":
                return (wd_l if lo else wd_h)[:, CB[g]:CB[g] + len(CH[g]), :]
            w = {"g": (wg_h, wg_l), "u": (wu_h, wu_l)}[kind][lo]
            return w[:, :, columns(kind, g)]

        def lo_on_pool(i):
            return units[i][0] == "u"

        DVE_UNITS = [i for i in range(12) if not lo_on_pool(i)]
        POOL_UNITS = [i for i in range(12) if lo_on_pool(i)]

        def wait_unit(eng, key):
            i = uidx[key]
            if lo_on_pool(i):
                eng.wait_ge(g_wl, POOL_UNITS.index(i) + 1)
            else:
                eng.wait_ge(v_wl, DVE_UNITS.index(i) + 1)

        def segments(g):
            lo, hi = GOFF[g], GOFF[g] + GWID[g]
            segs = [(0, SFF, None)] + [(SFF + e * EFF, SFF + (e + 1) * EFF, e) for e in range(NE)]
            return [(max(a, lo) - lo, min(b, hi) - max(a, lo), e) for a, b, e in segs if a < hi and b > lo]

        PROB_BANK = (3, 4, 3)
        WVO_BANK = (4, 5, 3, 4)

        def split3(mm, out_, lh, ll, rh, rl, start, stop, **kw):
            mm(out_, lh, rh, start=start, stop=False, **kw)
            mm(out_, lh, rl, start=False, stop=False, **kw)
            return mm(out_, ll, rh, start=False, stop=stop, **kw)

        block = ctx.enter_context(nc.Block())
        out_v = out.rearrange("b (h p) d -> p (b h) d", p=P)
        x_v = d["x"].rearrange("b (h p) d -> p (b h) d", p=P)

        def pairs(eng, first, last, body):
            body(first, first % 2, True, False)
            with eng.Fori(first + 1, last - 1, 2) as i:
                body(i, (first + 1) % 2, False, False)
                body(i + 1, first % 2, False, False)
            body(last, last % 2, False, True)

        @block.sync
        def _(sp):
            sp.dma_start(x[:, 0:2, :], x_v[:, 0:2, :]).then_inc(sp_x0, 16)
            for t_, s_ in ((ident, "ident"), (tri8, "tri8")):
                sp.dma_start(t_[tuple(slice(None) for _ in t_.shape)], d[s_]).then_inc(sp_c, 16)

            def load_unit(i):
                kind, g = units[i]
                if i >= NRING:
                    wait_unit(sp, units[i - NRING])
                if kind == "d":
                    n = sum(w == P for _, w in CH[g])
                    src = d["wd"][GOFF[g]:GOFF[g] + n * P, :].rearrange("(c p) n -> p c n", p=P)
                    sp.dma_start(unit_raw(i)[:, 0:n, :], src).then_inc(sp_w[i], 16)
                    if n < len(CH[g]):
                        w = CH[g][n][1]
                        sp.dma_start(unit_raw(i)[0:w, n, :], d["wd"][GOFF[g] + n * P:GOFF[g] + GWID[g], :]).then_inc(sp_w[i], 16)
                else:
                    src = d["w" + kind].rearrange("(k p) n -> p k n", p=P)[:, :, columns(kind, g)]
                    sp.dma_start(unit_raw(i), src).then_inc(sp_w[i], 16)

            for i in range(4):
                load_unit(i)
            sp.dma_start(x[:, 2:8, :], x_v[:, 2:8, :]).then_inc(sp_x, 16)
            for i in range(4, 12):
                load_unit(i)
            sp.dma_start(x[:, 8:NT, :], x_v[:, 8:NT, :]).then_inc(sp_x, 16)
            sp.dma_start(wqa_raw[:, :, :], d["wqa"].rearrange("(k p) n -> p k n", p=P)).then_inc(sp_qa, 16)
            for t_, s_ in ((mask, "mask"), (cos, "cos"), (sin, "sin"), (kvln_row, "kvln_row"), (kvln2, "kvln2"),
                           (qs, "qln")):
                sp.dma_start(t_[tuple(slice(None) for _ in t_.shape)], d[s_]).then_inc(sp_c2, 16)
            sp.wait_ge(v_wl, len(DVE_UNITS) + 1)
            sp.wait_ge(g_wl, len(POOL_UNITS))
            sp.dma_start(wqb_raw[:, :, 0:QLR], d["wqbn"]).then_inc(sp_a1, 16)
            sp.dma_start(wqb_raw[:, :, QLR:2 * P], d["wqbn"][:, :, P:QLR]).then_inc(sp_a1, 16)
            sp.dma_start(kvbk_raw[:, :, :], d["kvbk"]).then_inc(sp_a1, 16)
            sp.dma_start(rot1_raw[:, :, :], d["wqbp"][0:P]).then_inc(sp_a1, 16)
            for i in range(2):
                sp.dma_start(rot2_raw[64 * i:64 * i + 64, :, :], d["wqbp"][P:QLR]).then_inc(sp_a1, 16)
            kv = d["kvbv"].rearrange("p (h e) n -> p h e n", e=2)
            sp.dma_start(kvbv_raw[:, :, 0:64], kv[:, :, 0, :]).then_inc(sp_a2, 16)
            sp.dma_start(kvbv_raw[:, :, 128:192], kv[:, :, 1, :]).then_inc(sp_a2, 16)
            sp.dma_start(wo_raw[:, :, :], d["wo"]).then_inc(sp_a2, 16)
            done = 0
            for n in (6, 6, 3, 1):
                sp.wait_ge(v_x, NT + done + n)
                sp.dma_start(out_v[:, done:done + n, :], x[:, done:done + n, :]).then_inc(sp_out, 16)
                done += n
            sp.wait_ge(sp_out, 64)

        @block.tensor
        def _(pe):
            mm, tr = nc.tensor.matmul, nc.tensor.transpose

            def xt(t):
                pe.wait_ge(v_xn, t + 1)
                if not (isinstance(t, int) and t == 0):
                    pe.wait_ge(v_xl, t)
                for k in range(KH):
                    last = tr(B[7][:, k * P:(k + 1) * P], xn[:, 0, k * P:(k + 1) * P], ident[:, :])
                last.then_inc(t_xt, 1)

            def up(n, g, par, t):
                if g == 0:
                    pe.wait_ge(v_xl, t + 1)
                if not (isinstance(n, int) and n < 2):
                    pe.wait_ge(v_h, n - 1)
                for w_h, w_l, bank, kind, s_ in ((wg_h, wg_l, B[g % 2], "g", t_g), (wu_h, wu_l, B[2 + g % 2], "u", t_u)):
                    if isinstance(n, int) and n < NG:
                        wait_unit(pe, (kind, g))
                    c = columns(kind, g)
                    for k in range(KH):
                        last = split3(mm, bank[:, 0:c.stop - c.start], xh[par][:, k, :], xl[par][:, k, :],
                                      w_h[:, k, c], w_l[:, k, c], k == 0, k == KH - 1)
                    last.then_inc(s_, 1)

            def ffn(f):
                t0 = NT * f

                def ht(n, g):
                    pe.wait_ge(v_h, n + 1)
                    if not (isinstance(n, int) and n < 2):
                        pe.wait_ge(v_hl, n - 1)
                    for i, (c, w) in enumerate(CH[g]):
                        last = tr(B[4 + g % 2][0:w, i * P:(i + 1) * P], hid[:, g % 2, c:c + w], ident[:, :])
                    last.then_inc(t_ht, 1)

                def down(n, g, t):
                    pe.wait_ge(v_hl, n + 1)
                    if isinstance(n, int) and n < NG:
                        wait_unit(pe, ("d", g))
                    if g == 0 and not (isinstance(t, int) and t == 0):
                        pe.wait_ge(v_x, t)
                    for i, (c, w) in enumerate(CH[g]):
                        last = split3(mm, B[6][:, 0:HID], hth[0:w, g % 2, i, :], htl[0:w, g % 2, i, :],
                                      wd_h[0:w, CB[g] + i, :], wd_l[0:w, CB[g] + i, :],
                                      g == 0 and i == 0, g == NG - 1 and i == len(CH[g]) - 1)
                    last.then_inc(t_dn, 1)

                if f == 0:
                    pe.wait_ge(sp_c, 2 * 16)
                    xt(0)
                else:
                    pe.wait_ge(v_ux, NSEQ)

                def tile(i, par, first, last):
                    t = i + t0
                    n = t * NG
                    for g in range(NG):
                        if not (f == 1 and first and g < 2):
                            up(n + g, g, par, t)
                        if g == 2 and not last:
                            xt(t + 1)
                        if not (first and g == 0):
                            ht(n + g - 1, (g - 1) % NG)
                        if not (first and g < 2):
                            down(n + g - 2, (g - 2) % NG, t if g >= 2 else t - 1)

                pairs(pe, 0, NT - 1, tile)
                n = (t0 + NT) * NG
                ht(n - 1, NG - 1)
                down(n - 2, NG - 2, t0 + NT - 1)
                down(n - 1, NG - 1, t0 + NT - 1)

            def query_weights(c):
                for h in range(NH):
                    last = mm(B[2 * c + h // 8][:, (h % 8) * KVL:(h % 8 + 1) * KVL],
                              wqb_raw[:, h, c * P:(c + 1) * P], kvbk_raw[:, h, :], start=True, stop=True)
                    if h % 8 == 7:
                        last.then_inc(t_w, 1)

            def output_weights(q):
                for p in range(2 * q, 2 * q + 2):
                    for e in range(2):
                        last = mm(B[WVO_BANK[q]][:, (p % 2) * HID:(p % 2 + 1) * HID], kvbv_raw[:, p, 64 * e:64 * e + P],
                                  wo_raw[:, 2 * p + e, :], start=(e == 0), stop=(e == 1))
                last.then_inc(t_w, 1)

            def attention():
                def transpose_x(b):
                    pe.wait_ge(v_axn, b + 1)
                    for j in range(2):
                        for k in range(KH):
                            last = tr(B[6 + j][:, k * P:(k + 1) * P], xn[:, j, k * P:(k + 1) * P], ident[:, :])
                        last.then_inc(t_ax, 1)

                def down_projections(b):
                    for j in range(2):
                        pe.wait_ge(v_ax, 2 * b + j + 1)
                        for k in range(KH):
                            last = split3(mm, B[6 + j][:, 0:QA], xh[j][:, k, :], xl[j][:, k, :],
                                          wqa_h[:, k, :], wqa_l[:, k, :], k == 0, k == KH - 1)
                        last.then_inc(t_qa, 1)

                def transpose_latents(b):
                    pe.wait_ge(v_cq, b + 1)
                    for j in range(2):
                        for k in range(3):
                            last = tr(B[6 + j][:, k * P:(k + 1) * P], cq[:, j, k, :], ident[:, :])
                        last.then_inc(t_at, 1)

                def queries(gi, par, j):
                    cs = slice(512 * gi, 512 * gi + 512)
                    split3(mm, B[6 + j][:, :], th[par][:, 0, j, :], tl[par][:, 0, j, :], wq1_h[:, cs], wq1_l[:, cs],
                           True, False)
                    mm(B[6 + j][:, :], th[par][:, 1, j, :], wq2[:, cs], start=False, stop=False)
                    mm(B[6 + j][:, :], tl[par][:, 1, j, :], wq2[:, cs], start=False, stop=True).then_inc(t_q, 1)

                def transpose_queries(c, j):
                    pe.wait_ge(a_q, 2 * c + j + 1)
                    pe.wait_ge(g_q, 2 * c + j + 1)
                    for h in range(HG):
                        last = tr(B[6 + j][:, h * P:(h + 1) * P], qsb[:, j, h, :], ident[:, :])
                    last.then_inc(t_qt, 1)

                def queries_read(c, j):
                    if j == 0:
                        pe.wait_ge(a_qt, 2 * c + 1)
                    else:
                        pe.wait_ge(v_qt, c + 1)

                def scores(c, u, par):
                    j, heads, nk = (0, range(4), 1) if u == 0 else (1, range(2 * u - 2, 2 * u), 2)
                    queries_read(c, j)
                    if not (isinstance(c, int) and c == 0):
                        pe.wait_ge(a_e, 3 * c - 2 + u)
                    for i, h in enumerate(heads):
                        if u == 0:
                            last = mm(B[0][:, i * P:(i + 1) * P], qt0[:, h, :], kt0[par][:, :], start=True, stop=True)
                            continue
                        last = split3(mm, B[u][:, i * nk * P:(i + 1) * nk * P], qth[:, h, :], qtl[:, h, :],
                                      th[par][:, 2, :, :], tl[par][:, 2, :, :], True, True)
                    last.then_inc(t_s, 1)

                def transpose_probs(c, u):
                    pe.wait_ge(g_n, 3 * c + u + 1)
                    if u == 2:
                        pe.wait_ge(a_t, 3 * c + 1)
                    elif u == 0 and not (isinstance(c, int) and c == 0):
                        pe.wait_ge(a_t, 3 * c)
                    for i in range(4):
                        src = i if u == 0 else 2 * (i % 2) + i // 2
                        last = tr(B[PROB_BANK[u]][:, i * P:(i + 1) * P], prob[:, u, src * P:(src + 1) * P], ident[:, :])
                    last.then_inc(t_t, 1)

                def head_outputs(c, gi, par):
                    pe.wait_ge(a_t, 3 * c + 3)
                    o = B[4][:, :].rearrange("p (r q) -> p r q", r=2)
                    for e in range(2):
                        mm(o, vpad[par][0][:, 64 - 64 * e:192 - 64 * e],
                           pt0[:, e::2, :], start=(e == 0), stop=False, skip_group_check=True)
                    for e in range(2):
                        last = mm(o[:, :, P:SEQ], vpad[par][1][:, 64 - 64 * e:192 - 64 * e], pt1[:, e::2, :],
                                  start=False, stop=(e == 1), skip_group_check=True)
                    last.then_inc(t_o, 1)

                def out_projection(c, gi, b):
                    pe.wait_ge(v_o, c + 1)
                    if gi == 0 and not (isinstance(b, int) and b == 0):
                        pe.wait_ge(v_ux, b)
                    for j in range(2):
                        for r in range(2):
                            q = slice(j * P, (j + 1) * P)
                            last = split3(mm, B[5][:, j * HID:(j + 1) * HID], oth[gi % 2][:, r, q], otl[gi % 2][:, r, q],
                                          wvo_h[:, 2 * gi + r, :], wvo_l[:, 2 * gi + r, :],
                                          gi == 0 and j == 0 and r == 0, gi == NHG - 1 and r == 1,
                                          skip_group_check=True)
                    last.then_inc(t_p, 1)

                pe.wait_ge(sp_a1, 6 * 16)
                pe.wait_ge(v_pad, 1)
                pe.wait_ge(v_h, NT * NG)
                query_weights(0)
                transpose_x(0)
                down_projections(0)
                query_weights(1)
                pe.wait_ge(sp_a2, 3 * 16)
                output_weights(0)
                transpose_latents(0)
                pe.wait_ge(v_aw, 6)
                for j in range(2):
                    pe.wait_ge(v_at, j + 1)
                    queries(0, 0, j)
                output_weights(1)
                for j in range(2):
                    transpose_queries(0, j)

                def sequence(b, par, first, last):
                    for gi in range(NHG):
                        c = NHG * b + gi
                        end = last and gi == NHG - 1
                        if end:
                            queries_read(c, 1)
                            xt(NT)
                        if gi and not last:
                            queries_read(c, 1)
                            (transpose_x, down_projections, transpose_latents)[gi - 1](b + 1)
                        for u in range(NUNIT):
                            scores(c, u, par)
                        for j in range(2):
                            if end:
                                break
                            if gi == 0 or last:
                                queries_read(c, j)
                            else:
                                pe.wait_ge((v_ax, a_qa, v_at)[gi - 1], 2 * b + j + 3)
                            queries((gi + 1) % NHG, par if gi < NHG - 1 else 1 - par, j)
                        if first and gi == 0:
                            output_weights(2)
                            pe.wait_ge(v_aw, 7)
                            output_weights(3)
                        else:
                            head_outputs(c - 1, (gi - 1) % NHG, par if gi else 1 - par)
                        if not end:
                            transpose_queries(c + 1, 0)
                        if first and gi == 0:
                            pe.wait_ge(v_aw, 9)
                        transpose_probs(c, 0)
                        if not end:
                            transpose_queries(c + 1, 1)
                        if not (first and gi == 0):
                            out_projection(c - 1, (gi - 1) % NHG, b if gi else b - 1)
                        if first and gi == 0:
                            pe.wait_ge(v_aw, 10)
                        transpose_probs(c, 1)
                        transpose_probs(c, 2)

                pairs(pe, 0, NSEQ - 1, sequence)
                c = NHG * NSEQ - 1
                pe.wait_ge(a_e, 3 * c + 3)
                up(NT * NG, 0, 0, NT)
                head_outputs(c, NHG - 1, (NSEQ - 1) % 2)
                up(NT * NG + 1, 1, 0, NT)
                out_projection(c, NHG - 1, NSEQ - 1)

            ffn(0)
            attention()
            ffn(1)

        @block.scalar
        def _(act):
            copy, fn = nc.scalar.copy, nc.scalar.activation

            def high_xt(t, par):
                act.wait_ge(t_xt, t + 1)
                copy(xh[par][:, :, :], B[7][:, 0:HID].rearrange("p (k n) -> p k n", k=KH)).then_inc(a_xh, 1)

            def ffn(f):
                t0 = NT * f

                def high_hidden(n, g):
                    act.wait_ge(t_ht, n + 1)
                    if not (isinstance(n, int) and n < 2):
                        act.wait_ge(t_dn, n - 1)
                    full = sum(w == P for _, w in CH[g])
                    bank = B[4 + g % 2][:, :].rearrange("p (c n) -> p c n", n=P)
                    last = copy(hth[:, g % 2, 0:full, :], bank[:, 0:full, :])
                    if full < len(CH[g]):
                        w = CH[g][full][1]
                        last = copy(hth[0:w, g % 2, full, :], bank[0:w, full, :])
                    last.then_inc(a_hh, 1)

                def high_weights(*keys):
                    for key in keys:
                        i, (kind, g) = uidx[key], key
                        act.wait_ge(sp_w[i], 32 if kind == "d" and CH[g][-1][1] < P else 16)
                        src, dst = unit_raw(i), unit_dst(i, 0)
                        full = sum(w == P for _, w in CH[g]) if kind == "d" else KH
                        last = copy(dst[:, 0:full, :], src[:, 0:full, :])
                        if kind == "d" and full < len(CH[g]):
                            w = CH[g][full][1]
                            last = copy(dst[0:w, full, :], src[0:w, full, :])
                        last.then_inc(a_wh, 1)

                nc.scalar.preload_act_table(ACT.Silu)
                if f == 0:
                    high_xt(0, 0)
                    high_weights(*units[0:4])

                def tile(i, par, first, last):
                    t = i + t0
                    for g in range(NG):
                        n = t * NG + g
                        act.wait_ge(t_g, n + 1)
                        if not (isinstance(n, int) and n < 2):
                            act.wait_ge(v_h, n - 1)
                        c0 = extra("g", g)
                        if g == 0:
                            nc.scalar.activation(nl[:, :], B[0][:, 0:NE], ACT.Copy, scale=-1.0).then_inc(a_nl, 1)
                        fn(silu[:, g % 2, 0:GWID[g]], B[g % 2][:, c0:c0 + GWID[g]], ACT.Silu).then_inc(a_sl, 1)
                        if g == 2 and not last:
                            high_xt(t + 1, 1 - par)
                        if f == 0 and last and g < 2:
                            act.wait_ge(v_pad, 1)
                            w = (wq1_h, wq2)[g][:, :].rearrange("p (h n) -> p h n", h=NH)
                            fn(w[:, :, KVL:P], (rot1_raw, rot2_raw)[g][:, :, :], ACT.Copy,
                               scale=qs2[:, g:g + 1]).then_inc(a_w, 1)
                        if not (first and g == 0):
                            high_hidden(n - 1, (g - 1) % NG)
                        if f == 0 and first:
                            high_weights(*units[WCUT[g]:WCUT[g + 1]])
                    if f == 0 and first:
                        act.wait_ge(sp_qa, 16)
                        copy(wqa_h[:, :, :], wqa_raw[:, :, :]).then_inc(a_wh, 1)

                pairs(act, 0, NT - 1, tile)
                high_hidden((t0 + NT) * NG - 1, NG - 1)

            ffn(0)

            def attention():
                def high_x(b):
                    for j in range(2):
                        act.wait_ge(t_ax, 2 * b + j + 1)
                        copy(xh[j][:, :, :], B[6 + j][:, 0:HID].rearrange("p (k n) -> p k n", k=KH)).then_inc(a_ax, 1)

                def copy_latents(b):
                    for j in range(2):
                        act.wait_ge(t_qa, 2 * b + j + 1)
                        copy(qa[:, j, :], B[6 + j][:, 0:QA]).then_inc(a_qa, 1)

                def mean_squares(b):
                    act.wait_ge(a_qa, 2 * b + 2)
                    for j in range(2):
                        for i, (a, w) in enumerate(((0, QLR), (QLR, KVL))):
                            last = fn(cq[:, j, :, :].rearrange("p k n -> p (k n)")[:, a:a + w], qa[:, j, a:a + w], ACT.Square, scale=float(w) ** -0.5,
                                      accum_out=ms[:, j, i:i + 1])
                    last.then_inc(a_ms, 1)

                def high_latents(b, par):
                    for j in range(2):
                        act.wait_ge(t_at, 2 * b + j + 1)
                        if j == 0:
                            copy(kt0[par][:, :], B[6][:, 2 * P:3 * P])
                        copy(th[par][:, :, j, :], B[6 + j][:, 0:3 * P].rearrange("p (k n) -> p k n", k=3)).then_inc(a_at, 1)

                def copy_queries(c):
                    for j in range(2):
                        act.wait_ge(t_q, 2 * c + j + 1)
                        copy(qsb[:, j, :, 0:KVL],
                             B[6 + j][:, :].rearrange("p (h n) -> p h n", h=HG)[:, :, 0:KVL]).then_inc(a_q, 1)

                def high_queries(c, j):
                    act.wait_ge(t_qt, 2 * c + j + 1)
                    copy((qt0, qth)[j][:, :, :], B[6 + j][:, :].rearrange("p (h n) -> p h n", h=HG)).then_inc(a_qt, 1)

                def exponentials(c, u):
                    m = 3 * c + u
                    act.wait_ge(v_m, m + 1)
                    if not (isinstance(c, int) and c == 0):
                        act.wait_ge(t_t, m - 2)
                    nh = 4 if u == 0 else 2
                    w = 512 // nh
                    for i in range(nh):
                        last = fn(prob[:, u, i * w:(i + 1) * w], B[u][:, i * w:(i + 1) * w], ACT.Exp,
                                  bias=nmax[:, u, i:i + 1], accum_out=rsum[:, u, i:i + 1])
                    last.then_inc(a_e, 1)

                def copy_probs(c, u):
                    act.wait_ge(t_t, 3 * c + u + 1)
                    bank = B[PROB_BANK[u]][:, :].rearrange("p (h n) -> p h n", h=HG)
                    if u == 0:
                        last = copy(pt0[:, :, 0:P], bank)
                    else:
                        hs = slice(2 * u - 2, 2 * u)
                        copy(pt0[:, hs, P:SEQ], bank[:, 0:2, :])
                        last = copy(pt1[:, hs, :], bank[:, 2:4, :])
                    last.then_inc(a_t, 1)

                def high_outputs(c, gi):
                    act.wait_ge(t_o, c + 1)
                    copy(oth[gi % 2][:, :, :], B[4][:, :].rearrange("p (r q) -> p r q", r=2)).then_inc(a_o, 1)

                def high_query_weights(c):
                    w = (wq1_h, wq2)[c][:, :].rearrange("p (h n) -> p h n", h=NH)
                    for i in range(2):
                        act.wait_ge(t_w, 2 * c + i + 1)
                        fn(w[:, 8 * i:8 * i + 8, 0:KVL], B[2 * c + i][:, :].rearrange("p (h n) -> p h n", h=8), ACT.Copy,
                           scale=qs2[:, c:c + 1]).then_inc(a_w, 1)

                def high_output_weights(q):
                    act.wait_ge(t_w, 5 + q)
                    fn(wvo_h[:, 2 * q:2 * q + 2, :], B[WVO_BANK[q]][:, :].rearrange("p (r n) -> p r n", r=2), ACT.Copy,
                       scale=kvln2[:, 0:1]).then_inc(a_w, 1)

                nc.scalar.preload_act_table(ACT.Exp)
                high_x(0)
                high_query_weights(0)
                copy_latents(0)
                mean_squares(0)
                high_query_weights(1)
                high_output_weights(0)
                high_latents(0, 0)
                copy_queries(0)
                high_output_weights(1)
                high_queries(0, 0)
                high_queries(0, 1)

                def sequence(b, par, first, last):
                    for gi in range(NHG):
                        c = NHG * b + gi
                        end = last and gi == NHG - 1
                        if end:
                            high_xt(NT, 0)
                        if not last:
                            if gi == 1:
                                high_x(b + 1)
                            if gi == 2:
                                copy_latents(b + 1)
                                mean_squares(b + 1)
                            if gi == 3:
                                high_latents(b + 1, 1 - par)
                        exponentials(c, 0)
                        if not end:
                            copy_queries(c + 1)
                        exponentials(c, 1)
                        exponentials(c, 2)
                        if first and gi == 0:
                            high_output_weights(2)
                            high_output_weights(3)
                        else:
                            high_outputs(c - 1, (gi - 1) % NHG)
                        if not end:
                            high_queries(c + 1, 0)
                        copy_probs(c, 0)
                        if not end:
                            high_queries(c + 1, 1)
                        copy_probs(c, 1)
                        copy_probs(c, 2)

                pairs(act, 0, NSEQ - 1, sequence)
                high_outputs(NHG * NSEQ - 1, NHG - 1)

            attention()
            ffn(1)

        @block.vector
        def _(dve):
            V = nc.vector
            link = Link(dve, v_link)
            linked = [0]

            def minus(out_, a, hi):
                return V.tensor_tensor(out_, a, hi.bitcast(F32), ALU.subtract)

            def variance(t, t0):
                V.bn_stats(st6[:, :], x[:, t - t0, :]).then_inc(v_link, 1)
                link.n += 1
                dve.wait_ge(v_link, link.base + link.n)
                dve.sem_inc(v_turn, 1)
                link(V.bn_aggr(mv[:, :], st6[:, :]))
                V.tensor_scalar(ve[:, :], mv[:, 1:2], LN_EPS, None, ALU.add).then_inc(v_st, 1)

            def normalise_tile(t, t0):
                dve.wait_ge(g_rs, t + 1)
                V.tensor_scalar(xn[:, 0, :], x[:, t - t0, :], mv[:, 0:1], rstd[:, 0:1], ALU.subtract,
                                ALU.mult).then_inc(v_xn, 1)

            def low_xt(t, par):
                dve.wait_ge(a_xh, t + 1)
                minus(xl[par][:, :, :], B[7][:, 0:HID].rearrange("p (k n) -> p k n", k=KH),
                      xh[par][:, :, :]).then_inc(v_xl, 1)

            def middle(n, g, par, t):
                dve.wait_ge(t_u, n + 1)
                dve.wait_ge(a_sl, n + 1)
                if g == 1:
                    dve.wait_ge(v_wt, t + 1)
                if not (isinstance(n, int) and n < 2):
                    dve.wait_ge(t_ht, n - 1)
                for a, w, e in segments(g):
                    s_, u_ = silu[:, g % 2, a:a + w], B[2 + g % 2][:, a:a + w]
                    if e is None:
                        last = V.tensor_tensor(hid[:, g % 2, a:a + w], s_, u_, ALU.mult)
                    else:
                        last = V.scalar_tensor_tensor(hid[:, g % 2, a:a + w], s_, wgt[:, par, e:e + 1], u_,
                                                      ALU.mult, ALU.mult)
                last.then_inc(v_h, 1)

            def low_part(w_l, w_h, src, scale, n):
                dve.wait_ge(a_w, n)
                V.scalar_tensor_tensor(w_l, src, scale, w_h.bitcast(F32), ALU.mult, ALU.subtract).then_inc(v_aw, 1)

            def low_query_weights(c, part):
                r = slice(0, P) if c == 0 else slice(64, P)
                hi = (wq1_h, wq2)[c][:, :].rearrange("p (h n) -> p h n", h=NH)[r]
                lo = (wq1_l, wq2)[c][:, :].rearrange("p (h n) -> p h n", h=NH)[r]
                if part == 2:
                    cs, hs, src, n = slice(KVL, P), slice(0, NH), (rot1_raw, rot2_raw)[c][r], c + 1
                else:
                    cs, hs, n = slice(0, KVL), slice(8 * part, 8 * part + 8), 2 * c + part + 3
                    src = B[2 * c + part][r, :].rearrange("p (h n) -> p h n", h=8)
                low_part(lo[:, hs, cs], hi[:, hs, cs], src, qs2[r, c:c + 1], n)

            def ffn(f):
                t0 = NT * f

                def expert_weights(t, par):
                    dve.wait_ge(g_en, t + 1)
                    link(V.tensor_scalar(en1[:, :], en[:, :], 1.0, None, ALU.add))
                    link(V.reciprocal(sg[:, :], en1[:, :]))
                    other = sg[:, :].unsqueeze(1).broadcast_to([P, NE, NE])
                    own = sg[:, :].unsqueeze(2).broadcast_to([P, NE, NE])
                    V.tensor_tensor(cgt[:, :, :], other, own, ALU.is_gt)
                    link(V.tensor_tensor(cge[:, :, :], other, own, ALU.is_ge))
                    link(V.tensor_tensor(cgl[:, :, :], cge[:, :, :], tri8[:, :, :], ALU.mult))
                    link(V.tensor_tensor(cbt[:, :, :], cgl[:, :, :], cgt[:, :, :], ALU.max))
                    link(V.tensor_reduce(cnt[:, :], cbt[:, :, :], AX.X, ALU.add))
                    link(V.scalar_tensor_tensor(msk[:, :], cnt[:, :], 2.0, sg[:, :], ALU.is_lt, ALU.mult,
                                                accum_out=den[:, 0:1]))
                    link(V.tensor_scalar(den[:, 1:2], den[:, 0:1], 1e-20, None, ALU.add))
                    link(V.reciprocal(den[:, 2:3], den[:, 1:2]))
                    V.tensor_scalar(wgt[:, par, :], msk[:, :], den[:, 2:3], TOPK_SCALE, ALU.mult,
                                    ALU.mult).then_inc(v_wt, 1)

                def low_hidden(n, g):
                    dve.wait_ge(a_hh, n + 1)
                    full = sum(w == P for _, w in CH[g])
                    bank = B[4 + g % 2][:, :].rearrange("p (c n) -> p c n", n=P)
                    last = minus(htl[:, g % 2, 0:full, :], bank[:, 0:full, :], hth[:, g % 2, 0:full, :])
                    if full < len(CH[g]):
                        w = CH[g][full][1]
                        last = minus(htl[0:w, g % 2, full, :], bank[0:w, full, :], hth[0:w, g % 2, full, :])
                    last.then_inc(v_hl, 1)

                def add_to_x(t):
                    dve.wait_ge(t_dn, (t + 1) * NG)
                    V.scalar_tensor_tensor(x[:, t - t0, :], B[6][:, 0:HID], 0.5, x[:, t - t0, :], ALU.mult,
                                           ALU.add).then_inc(v_x, 1)

                def low_weights(*keys):
                    for kind, g in keys:
                        i = uidx[(kind, g)]
                        if lo_on_pool(i):
                            continue
                        dve.wait_ge(a_wh, i + 1)
                        src, hi, lo = unit_raw(i), unit_dst(i, 0), unit_dst(i, 1)
                        full = sum(w == P for _, w in CH[g]) if kind == "d" else KH
                        last = minus(lo[:, 0:full, :], src[:, 0:full, :], hi[:, 0:full, :])
                        if kind == "d" and full < len(CH[g]):
                            w = CH[g][full][1]
                            last = minus(lo[0:w, full, :], src[0:w, full, :], hi[0:w, full, :])
                        last.then_inc(v_wl, 1)

                link.at(linked[0])
                if f == 0:
                    variance(0, 0)
                    normalise_tile(0, 0)
                    low_xt(0, 0)
                    low_weights(*units[0:4])
                start = linked[0] + link.n
                per = 2 + 9

                def tile(i, par, first, last):
                    t = i + t0
                    link.at(i * per + start)
                    if f == 0 and last:
                        dve.wait_ge(sp_a1, 6 * 16)
                        dve.wait_ge(sp_a2, 3 * 16)
                        V.tensor_scalar(qs2[:, :], qs[:, :], SM_SCALE, None, ALU.mult)
                        V.tensor_tensor(kvbk_raw[:, :, :], kvbk_raw[:, :, :],
                                        kvln_row[:, :].unsqueeze(1).broadcast_to([P, NH, KVL]), ALU.mult)
                        V.memset(kvbv_raw[:, :, 64:128], 0.0).then_inc(v_pad, 1)
                    for g in range(NG):
                        n = t * NG + g
                        if not (f == 1 and first and g == 0):
                            middle(n, g, par, t)
                        if g == 1 and not last:
                            normalise_tile(t + 1, t0)
                        if g == 2 and not last:
                            low_xt(t + 1, 1 - par)
                        if not (first and g == 0):
                            low_hidden(n - 1, (g - 1) % NG)
                        if f == 0 and first:
                            low_weights(*units[WCUT[g]:WCUT[g + 1]])
                        if g == 0:
                            if not last:
                                variance(t + 1, t0)
                            expert_weights(t, par)
                        if g == 1 and not first:
                            add_to_x(t - 1)
                        if f == 0 and last and g < 2:
                            low_query_weights(g, 2)
                    assert last or link.n == per, link.n
                    if f == 0 and first:
                        dve.wait_ge(a_wh, len(units) + 1)
                        minus(wqa_l[:, :, :], wqa_raw[:, :, :], wqa_h[:, :, :]).then_inc(v_wl, 1)
                        dve.wait_ge(sp_x, 32)
                        dve.wait_ge(sp_c2, 6 * 16)

                pairs(dve, 0, NT - 1, tile)
                low_hidden((t0 + NT) * NG - 1, NG - 1)
                add_to_x(t0 + NT - 1)
                linked[0] = start + (NT - 1) * per + link.n

            V.memset(mhalf[:, :], -0.5)
            V.memset(ebase[:, :], float(np.e)).then_inc(v_one, 1)
            dve.wait_ge(sp_x0, 16)
            dve.wait_ge(sp_c, 2 * 16)
            ffn(0)

            def attention():
                def variances(b):
                    for j in range(2):
                        V.bn_stats(ast6[:, j, :], x[:, TPS * b + j, :]).then_inc(v_link, 1)
                    link.n += 2
                    dve.wait_ge(v_link, link.base + link.n)
                    dve.sem_inc(v_turn, 1)
                    for j in range(2):
                        V.bn_aggr(amv[:, j, :], ast6[:, j, :]).then_inc(v_link, 1)
                    link.n += 2
                    dve.wait_ge(v_link, link.base + link.n)
                    V.tensor_scalar(ave[:, :], amv[:, :, 1], LN_EPS, None, ALU.add).then_inc(v_ast, 1)

                def normalise(b):
                    dve.wait_ge(g_ars, b + 1)
                    for j in range(2):
                        last = V.tensor_scalar(xn[:, j, :], x[:, TPS * b + j, :], amv[:, j, 0:1], arstd[:, j:j + 1],
                                               ALU.subtract, ALU.mult)
                    last.then_inc(v_axn, 1)

                def low_x(b):
                    for j in range(2):
                        dve.wait_ge(a_ax, 2 * b + j + 1)
                        minus(xl[j][:, :, :], B[6 + j][:, 0:HID].rearrange("p (k n) -> p k n", k=KH),
                              xh[j][:, :, :]).then_inc(v_ax, 1)

                def squares_eps(b):
                    dve.wait_ge(a_ms, b + 1)
                    V.tensor_scalar(mse[:, :, :], ms[:, :, :], RMS_EPS, None, ALU.add).then_inc(v_ms, 1)

                def rotate_key(b):
                    dve.wait_ge(a_qa, 2 * b + 2)
                    half = DR // 2
                    kpe = qa[:, :, QLR + KVL:QA]
                    V.tensor_tensor(kr[:, :, 0, :], kpe, cos[:, :, :], ALU.mult)
                    V.tensor_tensor(kr[:, :, 1, 0:half], kpe[:, :, half:DR], sin[:, :, 0:half], ALU.mult)
                    link(V.tensor_tensor(kr[:, :, 1, half:DR], kpe[:, :, 0:half], sin[:, :, half:DR], ALU.mult))

                def latents(b, par):
                    dve.wait_ge(g_rr, b + 1)
                    for j in range(2):
                        r0, r1 = rr[:, j, 0:1], rr[:, j, 1:2]
                        flat = cq[:, j, :, :].rearrange("p k n -> p (k n)")
                        V.tensor_scalar(flat[:, 0:QLR], qa[:, j, 0:QLR], r0, None, ALU.mult)
                        V.tensor_scalar(flat[:, QLR:2 * P], qa[:, j, P:QLR], r0, None, ALU.mult)
                        V.tensor_scalar(flat[:, 2 * P:2 * P + KVL], qa[:, j, QLR:QLR + KVL], r1, None, ALU.mult)
                        V.tensor_scalar(vpad[par][j][:, KVL:2 * KVL], qa[:, j, QLR:QLR + KVL], r1, None, ALU.mult)
                    V.tensor_tensor(cq[:, :, 2, KVL:P], kr[:, :, 0, :], kr[:, :, 1, :], ALU.add).then_inc(v_cq, 1)

                def low_latents(b, par):
                    for j in range(2):
                        dve.wait_ge(a_at, 2 * b + j + 1)
                        minus(tl[par][:, :, j, :], B[6 + j][:, 0:3 * P].rearrange("p (k n) -> p k n", k=3),
                              th[par][:, :, j, :]).then_inc(v_at, 1)

                def rotate_queries(c):
                    half = DR // 2
                    for j in range(2):
                        dve.wait_ge(t_q, 2 * c + j + 1)
                        dve.wait_ge(a_q, 2 * c + j + 1)
                        pe_part = B[6 + j][:, :].rearrange("p (h n) -> p h n", h=HG)[:, :, KVL:P]

                        def table(tab, a, w):
                            return tab[:, j, a:a + w].unsqueeze(1).broadcast_to([P, HG, w])

                        V.tensor_tensor(qsb[:, j, :, KVL:P], pe_part, table(cos, 0, DR), ALU.mult)
                        V.tensor_tensor(rt2[:, j, :, 0:half], pe_part[:, :, half:DR], table(sin, 0, half), ALU.mult)
                        V.tensor_tensor(rt2[:, j, :, half:DR], pe_part[:, :, 0:half], table(sin, half, half),
                                        ALU.mult).then_inc(v_q, 1)

                def low_queries(c):
                    dve.wait_ge(a_qt, 2 * c + 2)
                    minus(qtl[:, :, :], B[7][:, :].rearrange("p (h n) -> p h n", h=HG), qth[:, :, :]).then_inc(v_qt, 1)

                def maxima(c, u):
                    dve.wait_ge(t_s, 3 * c + u + 1)
                    nh = 4 if u == 0 else 2
                    s_ = B[u][:, :].rearrange("p (h n) -> p h n", h=nh)
                    diag = s_ if u == 0 else s_[:, :, P:SEQ]
                    link(V.tensor_tensor(diag, diag, mask[:, :].unsqueeze(1).broadcast_to([P, nh, P]), ALU.add))
                    V.tensor_reduce(nmax[:, u, 0:nh], s_, AX.X, ALU.max, negate=True).then_inc(v_m, 1)

                def reciprocals(c, u):
                    dve.wait_ge(a_e, 3 * c + u + 1)
                    nh = 4 if u == 0 else 2
                    V.reciprocal(rcp[:, u, 0:nh], rsum[:, u, 0:nh]).then_inc(v_r, 1)

                def low_output_weights(q):
                    low_part(wvo_l[:, 2 * q:2 * q + 2, :], wvo_h[:, 2 * q:2 * q + 2, :],
                             B[WVO_BANK[q]][:, :].rearrange("p (r n) -> p r n", r=2), kvln2[:, 0:1], 7 + q)

                def low_outputs(c, gi):
                    dve.wait_ge(a_o, c + 1)
                    minus(otl[gi % 2][:, :, :], B[4][:, :].rearrange("p (r q) -> p r q", r=2),
                          oth[gi % 2][:, :, :]).then_inc(v_o, 1)

                def add_to_x(b):
                    dve.wait_ge(t_p, NHG * b + NHG)
                    V.tensor_tensor(x[:, bass.ds(TPS * b, TPS), :], B[5][:, :].rearrange("p (j n) -> p j n", j=TPS),
                                    x[:, bass.ds(TPS * b, TPS), :], ALU.add).then_inc(v_ux, 1)

                link.at(linked[0])
                variances(0)
                normalise(0)
                for i in range(2):
                    for j in range(2):
                        V.memset(vpad[i][j][:, 0:KVL], 0.0)
                        V.memset(vpad[i][j][:, 2 * KVL:3 * KVL], 0.0)
                low_x(0)
                low_query_weights(0, 0)
                low_query_weights(0, 1)
                rotate_key(0)
                squares_eps(0)
                low_query_weights(1, 0)
                latents(0, 0)
                low_query_weights(1, 1)
                low_output_weights(0)
                low_latents(0, 0)
                rotate_queries(0)
                low_output_weights(1)
                low_queries(0)
                start = linked[0] + link.n
                per = 5 + 3 * NHG

                def sequence(b, par, first, last):
                    link.at(b * per + start)
                    for gi in range(NHG):
                        c = NHG * b + gi
                        end = last and gi == NHG - 1
                        if last and gi == 0:
                            variance(NT, NT)
                        if end:
                            low_xt(NT, 0)
                        if not last:
                            if gi == 0:
                                variances(b + 1)
                            if gi == 1:
                                low_x(b + 1)
                            if gi == 3:
                                low_latents(b + 1, 1 - par)
                        for u in range(NUNIT):
                            maxima(c, u)
                            if u == 0 and gi == 2 and not last:
                                squares_eps(b + 1)
                        reciprocals(c, 0)
                        if not end:
                            rotate_queries(c + 1)
                        reciprocals(c, 1)
                        reciprocals(c, 2)
                        if gi == 2 and not last:
                            rotate_key(b + 1)
                        if first and gi == 0:
                            low_output_weights(2)
                            low_output_weights(3)
                        else:
                            low_outputs(c - 1, (gi - 1) % NHG)
                        if gi == 2 and not last:
                            latents(b + 1, 1 - par)
                        if not end:
                            low_queries(c + 1)
                        if gi == 0 and not last:
                            normalise(b + 1)
                        if gi == 0 and last:
                            normalise_tile(NT, NT)
                        if gi == 0 and not first:
                            add_to_x(b - 1)
                    assert last or link.n == per, link.n

                pairs(dve, 0, NSEQ - 1, sequence)
                low_outputs(NHG * NSEQ - 1, NHG - 1)
                middle(NT * NG, 0, 0, NT)
                add_to_x(NSEQ - 1)
                linked[0] = start + (NSEQ - 1) * per + link.n

            attention()
            dve.wait_ge(v_ux, NSEQ)
            ffn(1)

        @block.gpsimd
        def _(pool):
            G = nc.gpsimd

            def tile_rstd(t):
                pool.wait_ge(v_st, t + 1)
                G.tensor_tensor(rstd[:, :], ve[:, :], mhalf[:, 0:1], ALU.pow).then_inc(g_rs, 1)

            def ffn(f):
                t0 = NT * f

                def exp_of(t):
                    pool.wait_ge(a_nl, t + 1)
                    G.tensor_tensor(en[:, :], ebase[:, :], nl[:, :], ALU.pow).then_inc(g_en, 1)

                def low_weights(*keys):
                    for key in keys:
                        i = uidx[key]
                        if lo_on_pool(i):
                            pool.wait_ge(a_wh, i + 1)
                            G.tensor_tensor(unit_dst(i, 1), unit_raw(i), unit_dst(i, 0).bitcast(F32),
                                            ALU.subtract).then_inc(g_wl, 1)

                if f == 0:
                    tile_rstd(0)
                    low_weights(*units[0:4])

                def tile(i, par, first, last):
                    exp_of(i + t0)
                    if f == 0 and first:
                        low_weights(*units[WCUT[0]:WCUT[1]])
                    if not last:
                        tile_rstd(i + t0 + 1)
                    if f == 0 and first:
                        low_weights(*units[WCUT[1]:])

                pairs(pool, 0, NT - 1, tile)

            pool.wait_ge(v_one, 1)
            ffn(0)

            def attention():
                def rstd_of(b):
                    pool.wait_ge(v_ast, b + 1)
                    G.tensor_tensor(arstd[:, :], ave[:, :], mhalf[:, 0:2], ALU.pow).then_inc(g_ars, 1)

                def rms_of(b):
                    pool.wait_ge(v_ms, b + 1)
                    G.tensor_tensor(rr[:, :, :].rearrange("p j i -> p (j i)"), mse[:, :, :].rearrange("p j i -> p (j i)"),
                                    mhalf[:, 0:4], ALU.pow).then_inc(g_rr, 1)

                def add_rotation(c):
                    for j in range(2):
                        pool.wait_ge(v_q, 2 * c + j + 1)
                        G.tensor_tensor(qsb[:, j, :, KVL:P], qsb[:, j, :, KVL:P], rt2[:, j, :, :], ALU.add).then_inc(g_q, 1)

                def probabilities(c, u):
                    pool.wait_ge(v_r, 3 * c + u + 1)
                    nh = 4 if u == 0 else 2
                    place = prob[:, u, :].rearrange("p (h n) -> p h n", h=nh)
                    G.tensor_tensor(place, place, rcp[:, u, 0:nh].unsqueeze(2).broadcast_to([P, nh, 512 // nh]),
                                    ALU.mult).then_inc(g_n, 1)

                rstd_of(0)
                rms_of(0)
                add_rotation(0)

                def sequence(b, par, first, last):
                    for gi in range(NHG):
                        c = NHG * b + gi
                        if gi == 0:
                            if last:
                                tile_rstd(NT)
                            else:
                                rstd_of(b + 1)
                        if gi == 2 and not last:
                            rms_of(b + 1)
                        probabilities(c, 0)
                        if not (last and gi == NHG - 1):
                            add_rotation(c + 1)
                        probabilities(c, 1)
                        probabilities(c, 2)

                pairs(pool, 0, NSEQ - 1, sequence)

            attention()
            ffn(1)


def kernel(**inputs):
    import concourse.bacc as bacc
    from concourse.bass_utils import run_bass_kernel_spmd

    a = {k.replace("L0_", ""): np.asarray(v) for k, v in inputs.items()}
    qb = a["attn_w_qb"].reshape(NH, DN + DR, QLR)
    kvb = a["attn_w_kvb"].reshape(NH, DN + DV, KVL)
    qln, kvln = a["attn_q_a_ln_w"], a["attn_kv_a_ln_w"]
    inv = (np.float32(1.0) / np.float32(10000.0) ** (np.arange(0, DR, 2, dtype=np.float32) / np.float32(DR))).astype(np.float32)
    ang = np.outer(np.arange(SEQ, dtype=np.float32), inv).astype(np.float32)
    cos, sin = np.cos(ang), np.sin(ang)

    def tiles(t):
        return t.reshape(TPS, P, DR).transpose(1, 0, 2)

    arrays = {
        "x": a["attn_hidden_states"],
        "wg": np.concatenate([a["ffn_gate_w"], a["ffn_shared_wg"], a["ffn_exp_wg"].reshape(NE * EFF, HID)]).T,
        "wu": np.concatenate([a["ffn_shared_wu"], a["ffn_exp_wu"].reshape(NE * EFF, HID)]).T,
        "wd": np.concatenate([a["ffn_shared_wd"].T, a["ffn_exp_wd"].transpose(0, 2, 1).reshape(NE * EFF, HID)]),
        "wqa": np.concatenate([a["attn_w_qa"], a["attn_w_kva"]]).T,
        "wqbn": qb[:, :DN].transpose(1, 0, 2),
        "wqbp": qb[:, DN:].transpose(2, 0, 1),
        "kvbk": kvb[:, :DN].transpose(1, 0, 2),
        "kvbv": kvb[:, DN:].transpose(1, 0, 2),
        "wo": a["attn_w_o"].reshape(HID, NH, DV).transpose(2, 1, 0),
        "qln": np.stack([qln[0:P], np.concatenate([qln[P:QLR], qln[P:QLR]])], axis=1),
        "kvln2": np.concatenate([kvln, kvln])[:, None],
        "kvln_row": np.repeat(kvln[None, :], P, axis=0),
        "ident": np.eye(P, dtype=np.float32),
        "mask": np.where(np.arange(P)[None, :] <= np.arange(P)[:, None], 0.0, -1e30).astype(np.float32),
        "tri8": np.repeat(np.tri(NE, NE, -1, dtype=np.float32)[None], P, axis=0),
        "cos": tiles(np.concatenate([cos, cos], axis=1)),
        "sin": tiles(np.concatenate([-sin, sin], axis=1)),
    }
    arrays = {k: np.ascontiguousarray(v) for k, v in arrays.items()}
    nc = bacc.Bacc("TRN2", target_bir_lowering=False, num_devices=1, dynamic_dma_scratch_size=2048)
    d = {k: nc.dram_tensor("in_" + k, v.shape, F32, kind="ExternalInput").ap() for k, v in arrays.items()}
    out = nc.dram_tensor("out", arrays["x"].shape, F32, kind="ExternalOutput").ap()
    build(nc, d, out)
    r = run_bass_kernel_spmd(nc, [{"in_" + k: v for k, v in arrays.items()}], core_ids=[0])
    return r.results[0]["out"]
```
